# Optimizing a Trainium2 kernel written in Bass

```python
import numpy as np
import jax
import jax.numpy as jnp

def _softmax(x, axis=-1):
    return jax.nn.softmax(x, axis=axis)

def _gelu(x):
    return jax.nn.gelu(x, approximate=True)

def _silu(x):
    return jax.nn.silu(x)

def _sigmoid(x):
    return jax.nn.sigmoid(x)

def _layernorm(x, axis=-1, eps=1e-05):
    m = jnp.mean(x, axis=axis, keepdims=True)
    v = jnp.var(x, axis=axis, keepdims=True)
    return (x - m) / jnp.sqrt(v + eps)

def _scatter_add(tgt, idx, src, axis=0):
    return tgt.at[idx].add(src)

def _segment_sum(src, seg, n):
    return jax.ops.segment_sum(src, seg, n)
kernel_name = 'mk_adj_resnorm_d1_adj_r2_6a1ece'

def setup_inputs(seed: int=0):
    np.random.seed(seed)
    _w = jnp.asarray

    def _rec_inputs():
        import jax
        import jax.numpy as jnp
        _gk = jax.random.key(seed)
        x = -9.806e-05 + 1 * jax.random.normal(jax.random.fold_in(_gk, 1), (8192, 128), jnp.float32)
        _a = jax.random.bernoulli(jax.random.fold_in(_gk, 2), 0.00195312, (8192, 8192))
        _a = jnp.logical_or(_a, jnp.eye(8192, dtype=bool))
        _af = _a.astype(jnp.float32)
        adj = _af
        return (x, adj)
    x, adj = _rec_inputs()

    def _L0_gnn_setup():
        import jax, jax.numpy as jnp
        import numpy as np
        N, F_IN, HEADS, F_OUT = (2048, 128, 4, 32)
        DENSITY = 0.05
        key = jax.random.key(seed)
        k_x, k_adj, k_w, k_as, k_ad, k_b = jax.random.split(key, 6)
        x = jax.random.normal(k_x, (N, F_IN), dtype=jnp.float32)
        adj = (jax.random.uniform(k_adj, (N, N)) < DENSITY).astype(jnp.float32)
        adj = jnp.maximum(adj, jnp.eye(N, dtype=jnp.float32))
        weight = jax.random.normal(k_w, (HEADS * F_OUT, F_IN), dtype=jnp.float32) * 0.1
        att_src = jax.random.normal(k_as, (1, HEADS, F_OUT), dtype=jnp.float32) * 0.1
        att_dst = jax.random.normal(k_ad, (1, HEADS, F_OUT), dtype=jnp.float32) * 0.1
        bias = jax.random.normal(k_b, (HEADS * F_OUT,), dtype=jnp.float32) * 0.1
        return {'x': x, 'adj_matrix': adj, 'weight': weight, 'att_src': att_src, 'att_dst': att_dst, 'bias': bias}
    _L0_gnn_all = _L0_gnn_setup()
    _L0_gnn_in = {k: v for k, v in _L0_gnn_all.items() if k in ('weight', 'att_src', 'att_dst', 'bias')}
    del _L0_gnn_all
    return {'x': x, 'adj': adj, 'L0_gnn_weight': _L0_gnn_in['weight'], 'L0_gnn_att_src': _L0_gnn_in['att_src'], 'L0_gnn_att_dst': _L0_gnn_in['att_dst'], 'L0_gnn_bias': _L0_gnn_in['bias']}

def reference(x, adj, L0_gnn_weight, L0_gnn_att_src, L0_gnn_att_dst, L0_gnn_bias):
    import jax
    import jax.numpy as jnp

    def _L0_gnn_ref(x, adj_matrix, weight, att_src, att_dst, bias):
        import jax, jax.numpy as jnp
        import numpy as np
        N, F_IN, HEADS, F_OUT = (2048, 128, 4, 32)
        DENSITY = 0.05
        n = x.shape[0]
        heads = att_src.shape[1]
        f_out = weight.shape[0] // heads
        h_prime = (x @ weight.T).reshape(n, heads, f_out)
        alpha_src = jnp.sum(h_prime * att_src, axis=-1)
        alpha_dst = jnp.sum(h_prime * att_dst, axis=-1)
        C = alpha_src[None, :, :] + alpha_dst[:, None, :]
        adj_t = adj_matrix.T[..., None]
        tau = adj_t * jnp.exp(jnp.maximum(0.2 * C, C))
        tau_sum = jnp.sum(tau, axis=1, keepdims=True)
        att_weights = tau / tau_sum
        z = jnp.einsum('mnh,nhf->mhf', adj_t * att_weights, h_prime)
        return z.reshape(n, heads * f_out) + bias
    x = _layernorm(x + _L0_gnn_ref(x, adj, L0_gnn_weight, L0_gnn_att_src, L0_gnn_att_dst, L0_gnn_bias), axis=-1)
    return x

_drawn_inputs = setup_inputs


def setup_inputs(seed=0):
    import zlib

    import numpy as np

    out = dict(_drawn_inputs(seed))
    spreads = {}
    factors = {}
    for name, (base, spread) in spreads.items():
        noise = np.random.default_rng([zlib.crc32(name.encode()), seed]).standard_normal(out[name].shape)
        drawn = base * np.exp(spread * noise) if base else spread * noise
        out[name] = jnp.asarray(drawn.astype(out[name].dtype))
    for name, factor in factors.items():
        out[name] = (out[name] * factor).astype(out[name].dtype)
    return out
```

```python
import concourse.bass as bass
from concourse import mybir
from contextlib import ExitStack

F32 = mybir.dt.float32
F16 = mybir.dt.float16
F8 = mybir.dt.float8e4
U8 = mybir.dt.uint8
I8 = mybir.dt.int8
U32 = mybir.dt.uint32
ALU = mybir.AluOpType
ACT = mybir.ActivationFunctionType
AX = mybir.AxisListType


def gat_residual_layernorm(nc, x, adj, weight, att_src, att_dst, bias, out):
    P = 128
    N, FEAT = x.shape
    HEADS, FO = att_src.shape[1], att_src.shape[2]
    TILES = N // P
    GW = 512
    GROUPS = N // GW
    BLKS = GW // P
    UT = 2
    UNITS = TILES // UT
    SLOT_UNITS = 2
    LOADS = UNITS // SLOT_UNITS
    NSLOT = 4
    NMASK = 4
    BODY = NSLOT * SLOT_UNITS
    VW = FO + 1
    HL = 2 * VW
    HW = 2 * HL
    TW = HEADS * HW
    PW = HEADS * HL
    EW = PW + TW
    BANK = 512
    ONE8 = 0x38
    SPLIT = 2.0 ** 11
    TOP = 2.0 ** 14
    EPS = 1e-5
    HCOLS = HEADS * FO + 2 * HEADS
    CH = 4
    VT = 8
    def dve_pairs(u):
        return [(0, 0), (0, 1), (1, 0), (1, 1)] if u % 2 == 0 else [(0, 0), (0, 1), (1, 0)]

    def act_pairs(u):
        return [(j, h) for j in range(UT) for h in range(HEADS) if (j, h) not in dve_pairs(u)]

    x_t = x.rearrange("(t p) f -> p t f", p=P)
    out_t = out.rearrange("(t p) f -> p t f", p=P)
    adj_t = adj.rearrange("(t p) m -> p t m", p=P)
    d_rows = nc.dram_tensor("d_rows", (HEADS, N), F32, kind="Internal").ap()

    ctx = ExitStack()
    with ctx:
        def sb(name, shape, dt):
            return ctx.enter_context(nc.sbuf_tensor(name, shape, dt))

        def sem(name):
            return ctx.enter_context(nc.semaphore(name))

        vals = sb("vals", [P, TILES * TW], F16)
        ring = sb("ring", [P, TILES * HEADS * VW], F32)
        hp = ring[:, :].rearrange("p (t h v) -> p t h v", h=HEADS, v=VW)
        SLOT = SLOT_UNITS * UT * GW
        adj_in = ring[:, 0:NSLOT * SLOT].rearrange("p (s j m) -> p s j m", s=NSLOT, m=GW)
        mask = sb("mask", [P, NMASK, UT, HEADS, GW], U8)
        adj8 = sb("adj8", [P, NMASK, UT, GW], U8)
        d_bc = sb("d_bc", [P, 2 * HEADS * GW], F32)
        sums = sb("sums", [P, BLKS, EW], F32)
        num = sb("num", [P, BLKS, HEADS, VW], F32)
        rden = sb("rden", [P, BLKS, HEADS], F32)
        xres = sb("xres", [P, BLKS, FEAT], F32)
        y = sb("y", [P, BLKS, FEAT], F32)
        stats = sb("stats", [P, BLKS, 6], F32)
        mv = sb("mv", [P, BLKS, 2], F32)
        rstd = sb("rstd", [P, BLKS], F32)
        halfpow = sb("halfpow", [P, BLKS], F32)
        bias_bc = sb("bias_bc", [P, FEAT], F32)
        sd = sb("sd", [P, TILES, 2 * HEADS], F32)
        neg_s = sb("neg_s", [P, TILES * HEADS], F32)
        w_m = sb("w_m", [P, TILES * HEADS], F32)
        e1 = sb("e1", [P, TILES * HEADS], F32)
        e2 = sb("e2", [P, TILES * HEADS], F32)
        sp_ = sb("sp_", [P, TILES, HEADS], F32)
        dcol = sb("dcol", [P, HEADS, TILES], F32)
        dT = sb("dT", [P, 2, P], F32)
        habs = sb("habs", [P, TILES // CH * 2], F32)
        mx = sb("mx", [P, HEADS + 1], F32)
        mxa = sb("mxa", [P, HEADS + 1], F32)
        hscale = sb("hscale", [P, 1], F32)
        hscale2 = sb("hscale2", [P, 1], F32)
        ident = sb("ident", [P, P], F32)
        zeros16 = sb("zeros16", [P, P], F16)
        w_nat = sb("w_nat", [P, FEAT], F32)
        att = sb("att", [P, 2 * HEADS], F32)
        w_rhs = sb("w_rhs", [P, HCOLS], F32)
        xin = sb("xin", [P, 2, CH, FEAT], F32)
        xT = sb("xT", [P, 2, CH * P], F32)
        fval = sb("fval", [P, 2, VT * HEADS * VW], F32)

        ps = ctx.enter_context(nc.psum_tensor("ps", [P, 8, BANK], F32))

        w_loaded = sem("w_loaded")
        att_loaded = sem("att_loaded")
        bias_loaded = sem("bias_loaded")
        x_loaded = [sem(f"x_loaded{i}") for i in range(2)]
        a_loaded = [sem(f"a_loaded{i}") for i in range(NSLOT)]
        d_loaded = [sem(f"d_loaded{i}") for i in range(2)]
        xres_loaded = sem("xres_loaded")
        d_stored = sem("d_stored")
        out_stored = sem("out_stored")
        att_zeroed = sem("att_zeroed")
        consts_ready = sem("consts_ready")
        wT_ready = sem("wT_ready")
        wT_copied = sem("wT_copied")
        wa_ready = sem("wa_ready")
        wa_copied = sem("wa_copied")
        xin_free = sem("xin_free")
        xT_ready = sem("xT_ready")
        xT_copied = sem("xT_copied")
        h_ready = sem("h_ready")
        h_free = sem("h_free")
        dve_step = sem("dve_step")
        maxima_ready = sem("maxima_ready")
        maxima_all = sem("maxima_all")
        shifted = sem("shifted")
        exps_ready = sem("exps_ready")
        exps_scaled = sem("exps_scaled")
        dcol_ready = sem("dcol_ready")
        dT_ready = sem("dT_ready")
        dT_copied = sem("dT_copied")
        f1_ready = sem("f1_ready")
        f2_ready = sem("f2_ready")
        hi_ready = sem("hi_ready")
        lo_ready = sem("lo_ready")
        a_slot_free = sem("a_slot_free")
        adj8_ready = sem("adj8_ready")
        compares_done = sem("compares_done")
        signs_ready = sem("signs_ready")
        masks_ready = sem("masks_ready")
        mask_slots_free = sem("mask_slots_free")
        d_read_dve = sem("d_read_dve")
        d_read_act = sem("d_read_act")
        sums_done = sem("sums_done")
        evac_act = sem("evac_act")
        evac_dve = sem("evac_dve")
        sums_free = sem("sums_free")
        num_ready = sem("num_ready")
        rden_ready = sem("rden_ready")
        y_ready = sem("y_ready")
        stats_step = sem("stats_step")
        mv_ready = sem("mv_ready")
        pool_step = sem("pool_step")
        act_tick = sem("act_tick")
        dve_tick = sem("dve_tick")
        pe_tick = sem("pe_tick")
        pool_tick = sem("pool_tick")

        block = ctx.enter_context(nc.Block())

        @block.sync
        def _(sp):
            sp.dma_start(w_nat[:, :], weight).then_inc(w_loaded, 16)
            sp.dma_start(bias_bc[:, :], bias.partition_broadcast(P)).then_inc(bias_loaded, 16)
            with sp.Fori(0, TILES // CH // 2) as i:
                for b in range(2):
                    sp.wait_ge(xin_free, i * 2 + b + 1)
                    sp.dma_start(xin[:, b], x_t[:, bass.ds((i * 2 + b) * CH, CH), :]).then_inc(x_loaded[b], 16)
            sp.wait_ge(dT_copied, 1)
            for half in range(2):
                rows = d_rows.rearrange("h (t p) -> (h t) p", p=P)[half * P:(half + 1) * P, :]
                sp.dma_start(rows, dT[:, half, :]).then_inc(d_stored, 16)
            sp.wait_ge(d_stored, 32)

            def load_d(g, par):
                cols = d_rows[:, bass.ds(g * GW, GW)]
                sp.dma_start(d_bc[:, par * HEADS * GW:(par + 1) * HEADS * GW].rearrange("p (h m) -> p h m", h=HEADS),
                             cols.partition_broadcast(P)).then_inc(d_loaded[par], 16)

            with sp.Fori(0, GROUPS // 2) as g2:
                for par in range(2):
                    g = g2 * 2 + par
                    sp.wait_ge(d_read_dve, g + 1)
                    sp.wait_ge(d_read_act, g + 1)
                    load_d(g, par)
                    with sp.Fori(0, LOADS // NSLOT) as i:
                        k0 = i * NSLOT
                        for s in range(NSLOT):
                            sp.wait_ge(a_slot_free, g * LOADS + k0 + s + 1)
                            sp.dma_start(adj_in[:, s],
                                         adj_t[:, bass.ds((k0 + s) * SLOT_UNITS * UT, SLOT_UNITS * UT),
                                               bass.ds(g * GW, GW)]).then_inc(a_loaded[s], 16)

        @block.tensor
        def _(pe):
            pe.wait_ge(consts_ready, 1)
            pe.wait_ge(w_loaded, 16)
            nc.tensor.transpose(ps[:, 0, 0:P], w_nat[:, :], ident[:, :]).then_inc(wT_ready, 1)
            pe.wait_ge(att_loaded, 16 * 2 * HEADS)
            nc.tensor.matmul(ps[:, 1, 0:2 * HEADS], w_nat[:, :], att[:, :], start=True, stop=True).then_inc(wa_ready, 1)
            pe.wait_ge(wa_copied, 1)
            pe.wait_ge(wT_copied, 1)
            pe.sem_inc(xin_free, 2)
            with pe.Fori(0, TILES // CH // 2) as i:
                for b in range(2):
                    pe.wait_ge(x_loaded[b], i * 16 + 16)
                    for j in range(CH):
                        last = nc.tensor.transpose(ps[:, b, j * P:(j + 1) * P], xin[:, b, j, :], ident[:, :])
                    last.then_inc(xT_ready, 1)
                    pe.wait_ge(xT_copied, i * 2 + b + 1)
                    pe.wait_ge(h_free, i * 2 + b + 1)
                    for j in range(CH):
                        last = nc.tensor.matmul(ps[:, 2 + 2 * b + j // 2, (j % 2) * HCOLS:(j % 2 + 1) * HCOLS],
                                                xT[:, b, j * P:(j + 1) * P], w_rhs[:, :],
                                                start=True, stop=True)
                        if j == 0:
                            last.then_inc(xin_free, 1)
                    last.then_inc(h_ready, 1)
            pe.wait_ge(dcol_ready, 1)
            dflat = dcol[:, :, :].rearrange("p h t -> p (h t)")
            for half in range(2):
                last = nc.tensor.transpose(ps[:, 6, half * P:(half + 1) * P],
                                           dflat[:, half * P:(half + 1) * P], ident[:, :])
            last.then_inc(dT_ready, 1)
            pe.wait_ge(dT_copied, 1)
            pe.wait_ge(lo_ready, TILES // VT + 1)
            pe.wait_ge(hi_ready, 2 * TILES // VT + 2)
            pe.sem_inc(mask_slots_free, NMASK)

            with pe.Fori(0, GROUPS) as g:
                for b in range(BLKS):
                    pe.wait_ge(evac_act, BLKS * g + b + 1)
                    pe.wait_ge(evac_dve, BLKS * g + b + 1)
                    for k in range(2):
                        nc.tensor.matmul(ps[:, 2 * b + k, 0:1], zeros16[:, :], zeros16[:, 0:1],
                                         start=True, stop=False, skip_group_check=True)
                for u in range(UNITS):
                    q = u % NMASK
                    pe.wait_ge(masks_ready, g * UNITS + u + 1)
                    pe.sem_inc(pe_tick, 1)
                    for j in range(UT):
                        t = u * UT + j
                        heads = vals[:, t * TW:(t + 1) * TW].rearrange("p (h c) -> p h c", h=HEADS)
                        for b in range(BLKS):
                            m = slice(b * P, (b + 1) * P)
                            nc.tensor.matmul(ps[:, 2 * b, 0:PW].rearrange("p (h c) -> p h c", h=HEADS),
                                             adj8[:, q, j, m].bitcast(F8), heads[:, :, HL:HW],
                                             start=False, stop=False, skip_group_check=True)
                            for h in range(HEADS):
                                o = ps[:, 2 * b, PW:PW + HW] if h == 0 else ps[:, 2 * b + 1, (h - 1) * HW:h * HW]
                                last = nc.tensor.matmul(o, mask[:, q, j, h, m].bitcast(F8), heads[:, h, :],
                                                        start=False, stop=False, skip_group_check=True)
                    last.then_inc(mask_slots_free, 1)
                for b in range(BLKS):
                    for k in range(2):
                        last = nc.tensor.matmul(ps[:, 2 * b + k, 0:1], zeros16[:, :], zeros16[:, 0:1],
                                                start=False, stop=True, skip_group_check=True)
                last.then_inc(sums_done, 1)

        @block.scalar
        def _(act):
            with act.Fori(0, TILES // CH // 2) as i:
                for b in range(2):
                    act.wait_ge(xT_ready, i * 2 + b + 1)
                    act.wait_ge(h_free, i * 2 + b + 1)
                    nc.scalar.copy(xT[:, b, :], ps[:, b, :]).then_inc(xT_copied, 1)
            act.wait_ge(shifted, 1)
            sflat = sp_[:, :, :].rearrange("p t h -> p (t h)")
            nc.scalar.activation(e1[:, :], sflat, ACT.Exp)
            nc.scalar.activation(e2[:, :], sflat, ACT.Exp, scale=0.2)
            nc.scalar.activation(w_m[:, :], w_m[:, :], ACT.Exp, scale=0.8).then_inc(exps_ready, 1)
            act.sem_inc(hi_ready, 2)
            with act.Fori(0, TILES // VT) as i:
                for k, ready in ((0, f1_ready), (1, f2_ready)):
                    act.wait_ge(ready, i + 1)
                    v = vals[:, bass.ds(i * VT * TW, VT * TW)].rearrange("p (q s c) -> p q s c", s=2, c=HL)
                    nc.scalar.mul(v[:, :, k, 0:VW],
                                  fval[:, k, :].rearrange("p (q c) -> p q c", c=VW), 1.0 / SPLIT).then_inc(hi_ready, 1)

            def signs(g, u0, u, par):
                q = u % NMASK
                act.wait_ge(mask_slots_free, g * UNITS + u0 + u + 1)
                act.sem_inc(act_tick, 1)
                for j, h in act_pairs(u % 2):
                    last = nc.scalar.activation(
                        mask[:, q, j, h, :].bitcast(I8), d_bc[:, bass.ds(par * (HEADS * GW) + h * GW, GW)],
                        ACT.Sign, bias=neg_s[:, bass.ds(((u0 + u) * UT + j) * HEADS + h, 1)], scale=-1.0)
                last.then_inc(signs_ready, 1)

            def first_units(g, par, before):
                act.wait_ge(d_loaded[0], 16 * ((g + 2) // 2))
                if before is not None:
                    act.wait_ge(d_loaded[1], 16 * ((g + 1) // 2))
                for u in range(BODY):
                    signs(g, 0, u, par)
                    if u == 1 and before is not None:
                        act.wait_ge(sums_free, before + 1)
                        act.wait_ge(sums_done, before + 1)
                        for b in range(BLKS):
                            nc.scalar.copy(sums[:, b, 0:PW + HW], ps[:, 2 * b, 0:PW + HW]).then_inc(evac_act, 1)

            def other_units(g, par):
                with act.Fori(1, UNITS // BODY) as i:
                    u0 = i * BODY
                    for u in range(BODY):
                        signs(g, u0, u, par)
                act.drain().then_inc(d_read_act, 1)

            act.sem_inc(d_read_act, 2)
            act.sem_inc(evac_act, BLKS)
            first_units(0, 0, None)
            with act.Fori(0, GROUPS - 1) as g:
                other_units(g, g % 2)
                first_units(g + 1, (g + 1) % 2, g)
            other_units(GROUPS - 1, (GROUPS - 1) % 2)
            act.wait_ge(sums_free, GROUPS)
            act.wait_ge(sums_done, GROUPS)
            for b in range(BLKS):
                nc.scalar.copy(sums[:, b, 0:PW + HW], ps[:, 2 * b, 0:PW + HW]).then_inc(evac_act, 1)

        @block.vector
        def _(dve):
            steps = [0]

            def link(ins):
                steps[0] += 1
                ins.then_inc(dve_step, 1)
                dve.wait_ge(dve_step, steps[0])

            nc.vector.memset(zeros16[:, :], 0.0)
            nc.vector.memset(att[:, :], 0.0).then_inc(att_zeroed, 1)
            dve.wait_ge(wT_ready, 1)
            nc.vector.tensor_copy(w_rhs[:, 0:HEADS * FO], ps[:, 0, 0:P]).then_inc(wT_copied, 1)
            dve.wait_ge(wa_ready, 1)
            nc.vector.tensor_copy(w_rhs[:, HEADS * FO:HCOLS], ps[:, 1, 0:2 * HEADS]).then_inc(wa_copied, 1)
            dve.sem_inc(h_free, 2)
            with dve.Fori(0, TILES // CH // 2) as i:
                for b in range(2):
                    dve.wait_ge(h_ready, i * 2 + b + 1)
                    for k in range(2):
                        src = ps[:, 2 + 2 * b + k, 0:2 * HCOLS].rearrange("p (j c) -> p j c", j=2)
                        t0 = (i * 2 + b) * CH + 2 * k
                        nc.vector.tensor_copy(
                            ring[:, bass.ds(t0 * HEADS * VW, 2 * HEADS * VW)].rearrange("p (q v) -> p q v", v=VW)[:, :, 0:FO]
                            .rearrange("p (j h) v -> p j h v", h=HEADS),
                            src[:, :, 0:HEADS * FO].rearrange("p j (h v) -> p j h v", h=HEADS))
                        nc.vector.tensor_copy(sd[:, bass.ds(t0, 2), :], src[:, :, HEADS * FO:HCOLS])
                        last = nc.vector.tensor_reduce(habs[:, bass.ds((i * 2 + b) * 2 + k, 1)],
                                                       src[:, :, 0:HEADS * FO], axis=AX.XY, op=ALU.max,
                                                       apply_absolute_value=True)
                    last.then_inc(h_free, 1)
            dve.wait_ge(h_free, TILES // CH + 2)
            nc.vector.tensor_copy(dcol[:, :, :], sd[:, :, HEADS:2 * HEADS].rearrange("p t h -> p h t")).then_inc(dcol_ready, 1)
            nc.vector.tensor_reduce(mx[:, 0:HEADS], sd[:, :, 0:HEADS].rearrange("p t h -> p h t"), axis=AX.X, op=ALU.max)
            nc.vector.tensor_reduce(mx[:, HEADS:HEADS + 1], habs[:, :], axis=AX.X, op=ALU.max).then_inc(maxima_ready, 1)
            nc.vector.tensor_scalar(neg_s[:, :].rearrange("p (t h) -> p t h", h=HEADS), sd[:, :, 0:HEADS],
                                    -1.0, None, ALU.mult)
            dve.wait_ge(maxima_all, 1)
            smax = mxa[:, 0:HEADS].unsqueeze(1).to_broadcast([P, TILES, HEADS])
            nc.vector.tensor_tensor(sp_[:, :, :], sd[:, :, 0:HEADS], smax, ALU.subtract)
            nc.vector.tensor_tensor(w_m[:, :].rearrange("p (t h) -> p t h", h=HEADS), sd[:, :, HEADS:2 * HEADS],
                                    smax, ALU.add).then_inc(shifted, 1)
            link(nc.vector.tensor_scalar(hscale[:, :], mxa[:, HEADS:HEADS + 1], 1.0, None, ALU.max))
            link(nc.vector.reciprocal(hscale2[:, :], hscale[:, :]))
            link(nc.vector.tensor_scalar(hscale[:, :], hscale2[:, :], TOP * SPLIT, None, ALU.mult))
            dve.wait_ge(dT_ready, 1)
            nc.vector.tensor_copy(dT[:, :, :], ps[:, 6, 0:2 * P].rearrange("p (a b) -> p a b", a=2)).then_inc(dT_copied, 1)
            dve.wait_ge(exps_ready, 1)
            link(nc.vector.tensor_scalar(e1[:, :], e1[:, :], hscale[:, :], None, ALU.mult))
            nc.vector.tensor_scalar(e2[:, :], e2[:, :], hscale[:, :], None, ALU.mult).then_inc(exps_scaled, 1)
            dve.sem_inc(lo_ready, 1)
            with dve.Fori(0, TILES // VT) as i:
                dve.wait_ge(lo_ready, i + 1)
                dve.wait_ge(hi_ready, 2 * i + 2)
                nc.vector.tensor_tensor(
                    fval[:, 0, :].rearrange("p (q c) -> p q c", c=VW),
                    ring[:, bass.ds(i * VT * HEADS * VW, VT * HEADS * VW)].rearrange("p (q c) -> p q c", c=VW),
                    e1[:, bass.ds(i * VT * HEADS, VT * HEADS)].unsqueeze(2).to_broadcast([P, VT * HEADS, VW]),
                    ALU.mult).then_inc(f1_ready, 1)
                dve.wait_ge(hi_ready, 2 * i + 4)
                for k in range(2):
                    v = vals[:, bass.ds(i * VT * TW, VT * TW)].rearrange("p (q s c) -> p q s c", s=2, c=HL)
                    last = nc.vector.scalar_tensor_tensor(v[:, :, k, VW:HL], v[:, :, k, 0:VW], -SPLIT,
                                                          fval[:, k, :].rearrange("p (q c) -> p q c", c=VW),
                                                          ALU.mult, ALU.add)
                last.then_inc(lo_ready, 1)
            dve.wait_ge(f2_ready, TILES // VT)
            dve.wait_ge(lo_ready, TILES // VT + 1)
            dve.sem_inc(a_slot_free, NSLOT)
            dve.sem_inc(d_read_dve, 2)
            dve.sem_inc(evac_dve, BLKS)

            def unit(g, body, u, par):
                q, s = u % NMASK, u // SLOT_UNITS % NSLOT
                j0 = u % SLOT_UNITS * UT
                u0 = body * BODY
                done = g * UNITS + u0 + u
                dve.wait_ge(mask_slots_free, done + 1)
                if u % SLOT_UNITS == 0:
                    dve.wait_ge(a_loaded[s], 16 * (g * (LOADS // NSLOT) + body + 1))
                conv = nc.vector.tensor_scalar(adj8[:, q], adj_in[:, s, j0:j0 + UT, :], float(ONE8), None, ALU.mult)
                conv.then_inc(adj8_ready, 1)
                for j, h in dve_pairs(u % 2):
                    last = nc.vector.tensor_scalar(
                        mask[:, q, j, h, :], d_bc[:, bass.ds(par * (HEADS * GW) + h * GW, GW)],
                        neg_s[:, bass.ds(((u0 + u) * UT + j) * HEADS + h, 1)], float(ONE8), ALU.is_gt, ALU.mult)
                last.then_inc(compares_done, 1)
                if u % SLOT_UNITS == SLOT_UNITS - 1:
                    dve.wait_ge(adj8_ready, done + 1)
                    dve.sem_inc(a_slot_free, 1)
                dve.wait_ge(signs_ready, done + 1)
                dve.wait_ge(adj8_ready, done + 1)
                dve.wait_ge(compares_done, done + 1)
                words = mask[:, q].rearrange("p j h m -> p (j h m)").bitcast(U32).rearrange(
                    "p (j h m) -> p j h m", j=UT, h=HEADS)
                a = adj8[:, q].rearrange("p j m -> p (j m)").bitcast(U32).rearrange("p (j m) -> p j m", j=UT)
                a = a.unsqueeze(2).to_broadcast([P, UT, HEADS, GW // 4])
                nc.vector.tensor_tensor(words, words, a, ALU.bitwise_and).then_inc(masks_ready, 1)

            def evacuate(g):
                dve.wait_ge(sums_free, g + 1)
                dve.wait_ge(sums_done, g + 1)
                for b in range(BLKS):
                    nc.vector.tensor_copy(sums[:, b, PW + HW:EW], ps[:, 2 * b + 1, 0:3 * HW]).then_inc(evac_dve, 1)

            def denominators(g):
                dve.wait_ge(num_ready, g + 1)
                nc.vector.reciprocal(rden[:, :, :], num[:, :, :, FO]).then_inc(rden_ready, 1)

            def moments(g):
                dve.wait_ge(y_ready, g + 1)
                for b in range(BLKS):
                    last = nc.vector.bn_stats(stats[:, b, :], y[:, b, :])
                last.then_inc(stats_step, 1)
                dve.wait_ge(stats_step, g + 1)
                dve.sem_inc(dve_tick, 1)
                for b in range(BLKS):
                    last = nc.vector.bn_aggr(mv[:, b, :], stats[:, b, :])
                last.then_inc(mv_ready, 1)

            def first_units(g, par, before):
                dve.wait_ge(d_loaded[0], 16 * ((g + 2) // 2))
                if before is not None:
                    dve.wait_ge(d_loaded[1], 16 * ((g + 1) // 2))
                for u in range(BODY):
                    unit(g, 0, u, par)
                    if before is not None:
                        if u == 1:
                            evacuate(before)
                        if u == 4:
                            denominators(before)
                        if u == 7:
                            moments(before)

            def other_units(g, par):
                with dve.Fori(1, UNITS // BODY) as i:
                    for u in range(BODY):
                        unit(g, i, u, par)
                dve.wait_ge(masks_ready, g * UNITS + UNITS)
                dve.sem_inc(d_read_dve, 1)

            first_units(0, 0, None)
            with dve.Fori(0, GROUPS - 1) as g:
                other_units(g, g % 2)
                first_units(g + 1, (g + 1) % 2, g)
            other_units(GROUPS - 1, (GROUPS - 1) % 2)
            evacuate(GROUPS - 1)
            denominators(GROUPS - 1)
            moments(GROUPS - 1)

        @block.gpsimd
        def _(pool):
            nc.gpsimd.memset(ident[:, :], 0.0).then_inc(pool_step, 1)
            pool.wait_ge(pool_step, 1)
            nc.gpsimd.affine_select(out=ident[:, :], in_=ident[:, :], compare_op=ALU.not_equal, fill=1.0, base=0,
                                    pattern=[[-1, P]], channel_multiplier=1).then_inc(consts_ready, 1)
            pool.wait_ge(att_zeroed, 1)
            for k, a in enumerate((att_src, att_dst)):
                for h in range(HEADS):
                    pool.dma_start(att[h * FO:(h + 1) * FO, k * HEADS + h:k * HEADS + h + 1],
                                   a[0, h, :].unsqueeze(1)).then_inc(att_loaded, 16)
            nc.gpsimd.memset(halfpow[:, :], -0.5)
            nc.gpsimd.memset(hp[:, :, :, FO:VW].rearrange("p t h v -> p (t h) v"), 1.0).then_inc(pool_step, 1)
            pool.wait_ge(maxima_ready, 1)
            nc.gpsimd.partition_all_reduce(mxa[:, :], mx[:, :], P, bass.bass_isa.ReduceOp.max).then_inc(maxima_all, 1)
            pool.wait_ge(exps_scaled, 1)
            with pool.Fori(0, TILES // VT) as i:
                pool.wait_ge(lo_ready, i + 1)
                pool.wait_ge(hi_ready, 2 * i + 2)
                nc.gpsimd.tensor_tensor(
                    fval[:, 1, :].rearrange("p (q c) -> p q c", c=VW),
                    ring[:, bass.ds(i * VT * HEADS * VW, VT * HEADS * VW)].rearrange("p (q c) -> p q c", c=VW),
                    e2[:, bass.ds(i * VT * HEADS, VT * HEADS)].unsqueeze(2).to_broadcast([P, VT * HEADS, VW]),
                    ALU.mult).then_inc(f2_ready, 1)
            pool.wait_ge(bias_loaded, 16)

            pool.sem_inc(sums_free, 1)
            PRE, CHAIN = 2, 10
            with pool.Fori(0, GROUPS) as g:
                step = [0]

                def link(ins):
                    step[0] += 1
                    ins.then_inc(pool_step, 1)
                    pool.wait_ge(pool_step, g * CHAIN + PRE + step[0])
                    pool.sem_inc(pool_tick, 1)

                pool.dma_start(xres[:, :, :], x_t[:, bass.ds(g * BLKS, BLKS), :]).then_inc(xres_loaded, 16)
                pool.wait_ge(xres_loaded, g * 16 + 16)
                link(nc.gpsimd.tensor_tensor(xres[:, :, :], xres[:, :, :],
                                             bias_bc[:, :].unsqueeze(1).to_broadcast([P, BLKS, FEAT]), ALU.add))
                pool.wait_ge(evac_act, BLKS * g + 2 * BLKS)
                pool.wait_ge(evac_dve, BLKS * g + 2 * BLKS)
                adj_sum = sums[:, :, 0:PW].rearrange("p b (h c) -> p b h c", h=HEADS)
                head_sums = sums[:, :, PW:EW].rearrange("p b (h c) -> p b h c", h=HEADS)
                w = w_m[:, bass.ds(g * (BLKS * HEADS), BLKS * HEADS)].rearrange("p (b h) -> p b h", h=HEADS)
                w = w.unsqueeze(3).to_broadcast([P, BLKS, HEADS, HL])
                link(nc.gpsimd.tensor_tensor(adj_sum, adj_sum, head_sums[:, :, :, HL:HW], ALU.subtract))
                link(nc.gpsimd.tensor_tensor(head_sums[:, :, :, 0:HL], head_sums[:, :, :, 0:HL], w, ALU.mult))
                link(nc.gpsimd.tensor_tensor(adj_sum, adj_sum, head_sums[:, :, :, 0:HL], ALU.add))
                link(nc.gpsimd.tensor_scalar(adj_sum[:, :, :, VW:HL], adj_sum[:, :, :, VW:HL], 1.0 / SPLIT, None, ALU.mult))
                nc.gpsimd.tensor_tensor(num[:, :, :, :], adj_sum[:, :, :, 0:VW], adj_sum[:, :, :, VW:HL],
                                        ALU.add).then_inc(num_ready, 1)
                pool.wait_ge(num_ready, g + 1)
                pool.sem_inc(sums_free, 1)
                pool.wait_ge(rden_ready, g + 1)
                yh = y[:, :, :].rearrange("p b (h v) -> p b h v", h=HEADS)
                link(nc.gpsimd.tensor_tensor(yh, num[:, :, :, 0:FO],
                                             rden[:, :, :].unsqueeze(3).to_broadcast([P, BLKS, HEADS, FO]), ALU.mult))
                nc.gpsimd.tensor_tensor(y[:, :, :], y[:, :, :], xres[:, :, :], ALU.add).then_inc(y_ready, 1)
                pool.wait_ge(mv_ready, g + 1)
                pool.wait_ge(y_ready, g + 1)
                pool.sem_inc(pool_tick, 1)
                link(nc.gpsimd.tensor_scalar(rstd[:, :], mv[:, :, 1], EPS, None, ALU.add))
                link(nc.gpsimd.tensor_tensor(rstd[:, :], rstd[:, :], halfpow[:, :], ALU.pow))
                link(nc.gpsimd.tensor_tensor(y[:, :, :], y[:, :, :],
                                             mv[:, :, 0:1].to_broadcast([P, BLKS, FEAT]), ALU.subtract))
                link(nc.gpsimd.tensor_tensor(y[:, :, :], y[:, :, :],
                                             rstd[:, :].unsqueeze(2).to_broadcast([P, BLKS, FEAT]), ALU.mult))
                assert step[0] == CHAIN
                pool.dma_start(out_t[:, bass.ds(g * BLKS, BLKS), :], y[:, :, :]).then_inc(out_stored, 16)
                pool.wait_ge(out_stored, 16 * g + 16)


_INS = ["x", "adj", "L0_gnn_weight", "L0_gnn_att_src", "L0_gnn_att_dst", "L0_gnn_bias"]


def kernel(**inputs):
    import numpy as np
    import concourse.bacc as bacc
    from concourse.bass_utils import run_bass_kernel_spmd

    nc = bacc.Bacc("TRN2", target_bir_lowering=False, num_devices=1)
    arrays, args = {}, []
    for name in _INS:
        a = np.ascontiguousarray(inputs[name])
        arrays[f"in_{name}"] = a
        args.append(nc.dram_tensor(f"in_{name}", a.shape, mybir.dt.from_np(a.dtype), kind="ExternalInput").ap())
    shape = arrays["in_x"].shape
    args.append(nc.dram_tensor("out", shape, mybir.dt.from_np(np.dtype("float32")), kind="ExternalOutput").ap())
    gat_residual_layernorm(nc, *args)
    r = run_bass_kernel_spmd(nc, [arrays], core_ids=[0])
    return r.results[0]["out"]
```

```python
import concourse.bass as bass
from concourse import mybir
from contextlib import ExitStack

F32 = mybir.dt.float32
F16 = mybir.dt.float16
F8 = mybir.dt.float8e4
U8 = mybir.dt.uint8
BF16 = mybir.dt.bfloat16
I32 = mybir.dt.int32
ALU = mybir.AluOpType
ACT = mybir.ActivationFunctionType
AX = mybir.AxisListType


def gat_residual_layernorm(nc, x, adj, weight, att_src, att_dst, bias, out):
    P = 128
    N, FEAT = x.shape
    HEADS, FO = att_src.shape[1], att_src.shape[2]
    TILES = N // P
    GW = 512
    GROUPS = N // GW
    BLKS = GW // P
    UT = 2
    UNITS = TILES // UT
    SLOT_UNITS = 2
    LOADS = UNITS // SLOT_UNITS
    NSLOT = 4
    NMASK = 8
    BODY = NSLOT * SLOT_UNITS
    VW = FO + 1
    HL = 2 * VW
    HW = 2 * HL
    TW = HEADS * HW
    PW = HEADS * HL
    EW = PW + TW
    BANK = 512
    FLAG = [2.0, 1.0, 1.0, 1.0]
    WORD = 32.0
    INV = [0.5, 8.0, 8.0, 8.0]
    STEEP = 2.0 ** 40
    SPLIT = 2.0 ** 11
    TOP = 2.0 ** 14
    EPS = 1e-5
    EVAC_DVE, EVAC_ACT = 2, 5
    DVE_FOUR = (0, 2, 4, 6, 7)
    HCOLS = HEADS * FO + 2 * HEADS
    CH = 4
    VT = 4
    def dve_pairs(u):
        return [(0, 0), (1, 0), (0, 1)] + ([(1, 1)] if u % 8 in DVE_FOUR else [])

    def act_pairs(u):
        return [(j, h) for j in range(UT) for h in range(HEADS) if (j, h) not in dve_pairs(u)]

    x_t = x.rearrange("(t p) f -> p t f", p=P)
    out_t = out.rearrange("(t p) f -> p t f", p=P)
    adj_t = adj.rearrange("(t p) m -> p t m", p=P)
    d_rows = nc.dram_tensor("d_rows", (HEADS, N), F32, kind="Internal").ap()

    ctx = ExitStack()
    with ctx:
        def sb(name, shape, dt):
            return ctx.enter_context(nc.sbuf_tensor(name, shape, dt))

        def sem(name):
            return ctx.enter_context(nc.semaphore(name))

        vals = sb("vals", [P, TILES * TW], F16)
        SLOT = SLOT_UNITS * UT * GW
        ring = sb("ring", [P, NSLOT * SLOT], F32)
        adj_in = ring[:, :].rearrange("p (s j m) -> p s j m", s=NSLOT, m=GW)
        hp = sb("hp", [P, TILES * HEADS * VW], F32)
        mask = hp[:, 0:NMASK * UT * GW]
        words = mask.bitcast(I32).rearrange("p (q j m) -> p q j m", q=NMASK, j=UT)
        flags = mask.bitcast(U8).rearrange("p (q j m h) -> p q j h m", q=NMASK, j=UT, h=HEADS)
        mask8 = mask.bitcast(F8).rearrange("p (q j m h) -> p q j h m", q=NMASK, j=UT, h=HEADS)
        adj16 = ring[:, :].bitcast(BF16).rearrange("p (s j m two) -> p s j m two", s=NSLOT, m=GW, two=2)[:, :, :, :, 1]
        d_bc = sb("d_bc", [P, 2 * HEADS * GW], F32)
        sum_adj = sb("sum_adj", [P, BLKS, HEADS, HL], F32)
        sum_head = sb("sum_head", [P, BLKS, HEADS, HW], F32)
        num = sb("num", [P, BLKS * HEADS, VW], F32)
        num1 = sb("num1", [P, BLKS * HEADS, VW], F32)
        rden = sb("rden", [P, BLKS * HEADS], F32)
        xres = sb("xres", [P, 2 * BLKS * FEAT], F32)
        y = sb("y", [P, BLKS, FEAT], F32)
        stats = sb("stats", [P, BLKS, 6], F32)
        mv = sb("mv", [P, BLKS, 2], F32)
        rstd = sb("rstd", [P, BLKS], F32)
        halfpow = sb("halfpow", [P, BLKS], F32)
        bias_bc = sb("bias_bc", [P, FEAT], F32)
        sd = sb("sd", [P, TILES, 2 * HEADS], F32)
        big_s = sb("big_s", [P, TILES * HEADS], F32)
        neg_s = sb("neg_s", [P, TILES * HEADS], F32)
        w_log = sb("w_log", [P, TILES * HEADS], F32)
        w_m = sb("w_m", [P, TILES * HEADS], F32)
        e1 = sb("e1", [P, TILES * HEADS], F32)
        e2 = sb("e2", [P, TILES * HEADS], F32)
        sp_ = sb("sp_", [P, TILES, HEADS], F32)
        dcol = sb("dcol", [P, HEADS, TILES], F32)
        dT = sb("dT", [P, 2, P], F32)
        habs = sb("habs", [P, TILES // CH], F32)
        mx = sb("mx", [P, HEADS + 1], F32)
        mxa = sb("mxa", [P, HEADS + 1], F32)
        hscale = sb("hscale", [P, 1], F32)
        hscale2 = sb("hscale2", [P, 1], F32)
        ident = sb("ident", [P, P], F32)
        zeros16 = sb("zeros16", [P, P], F16)
        w_nat = sb("w_nat", [P, FEAT], F32)
        att = sb("att", [P, 2 * HEADS], F32)
        w_rhs = sb("w_rhs", [P, HCOLS], F32)
        FV = VT * HEADS * VW
        fbuf = sb("fbuf", [P, 4 * FV], F32)
        fval = fbuf[:, :].rearrange("p (b k c) -> p b k c", b=2, k=2)
        xT = fbuf[:, 0:2 * CH * P].rearrange("p (b n) -> p b n", b=2)
        XLOADS = 4

        ps = ctx.enter_context(nc.psum_tensor("ps", [P, 8, BANK], F32))

        w_loaded = sem("w_loaded")
        att_loaded = sem("att_loaded")
        bias_loaded = sem("bias_loaded")
        x_loaded = sem("x_loaded")
        a_loaded = [sem(f"a_loaded{i}") for i in range(NSLOT)]
        d_loaded = [sem(f"d_loaded{i}") for i in range(2)]
        xres_loaded = [sem(f"xres_loaded{i}") for i in range(2)]
        d_stored = sem("d_stored")
        out_stored = sem("out_stored")
        att_zeroed = sem("att_zeroed")
        consts_ready = sem("consts_ready")
        wT_ready = sem("wT_ready")
        wT_copied = sem("wT_copied")
        wa_ready = sem("wa_ready")
        wa_copied = sem("wa_copied")
        xT_ready = sem("xT_ready")
        xT_copied = sem("xT_copied")
        h_ready = sem("h_ready")
        h_free = sem("h_free")
        habs_ready = sem("habs_ready")
        dve_step = sem("dve_step")
        maxima_ready = sem("maxima_ready")
        maxima_all = sem("maxima_all")
        shifted = sem("shifted")
        exps_ready = sem("exps_ready")
        exps_scaled = sem("exps_scaled")
        dcol_ready = sem("dcol_ready")
        dT_ready = sem("dT_ready")
        dT_copied = sem("dT_copied")
        f1_ready = sem("f1_ready")
        f2_ready = sem("f2_ready")
        hi_ready = sem("hi_ready")
        lo_ready = sem("lo_ready")
        compares_done = sem("compares_done")
        signs_ready = sem("signs_ready")
        masks_ready = sem("masks_ready")
        units_done = sem("units_done")
        d_read_dve = sem("d_read_dve")
        d_read_act = sem("d_read_act")
        sums_done = sem("sums_done")
        evac_act = sem("evac_act")
        evac_dve = sem("evac_dve")
        sums_free = sem("sums_free")
        xres_free = sem("xres_free")
        var_ready = sem("var_ready")
        rstd_ready = sem("rstd_ready")
        y_ready = sem("y_ready")
        y_free = sem("y_free")
        final_step = sem("final_step")
        pool_step = sem("pool_step")
        act_tick = sem("act_tick")
        dve_tick = sem("dve_tick")
        pe_tick = sem("pe_tick")
        pool_tick = sem("pool_tick")

        block = ctx.enter_context(nc.Block())

        @block.sync
        def _(sp):
            sp.dma_start(w_nat[:, :], weight).then_inc(w_loaded, 16)
            sp.dma_start(bias_bc[:, :], bias.partition_broadcast(P)).then_inc(bias_loaded, 16)
            for k in range(XLOADS):
                t = TILES // XLOADS
                sp.dma_start(ring[:, k * t * FEAT:(k + 1) * t * FEAT].rearrange("p (t f) -> p t f", f=FEAT),
                             x_t[:, k * t:(k + 1) * t, :]).then_inc(x_loaded, 16)
            sp.wait_ge(dT_copied, 1)
            for half in range(2):
                rows = d_rows.rearrange("h (t p) -> (h t) p", p=P)[half * P:(half + 1) * P, :]
                sp.dma_start(rows, dT[:, half, :]).then_inc(d_stored, 16)
            sp.wait_ge(d_stored, 32)

            def load_group(g, par):
                sp.wait_ge(d_read_dve, g + 1)
                sp.wait_ge(d_read_act, g + 1)
                sp.dma_start(d_bc[:, par * HEADS * GW:(par + 1) * HEADS * GW].rearrange("p (h m) -> p h m", h=HEADS),
                             d_rows[:, bass.ds(g * GW, GW)].partition_broadcast(P)).then_inc(d_loaded[par], 16)
                sp.wait_ge(xres_free, g + 1)
                sp.dma_start(xres[:, par * BLKS * FEAT:(par + 1) * BLKS * FEAT].rearrange("p (b f) -> p b f", b=BLKS),
                             x_t[:, bass.ds(g * BLKS, BLKS), :]).then_inc(xres_loaded[par], 16)

            def load_adj(g, i):
                for s in range(NSLOT):
                    k = i * NSLOT + s
                    sp.wait_ge(units_done, (g * LOADS + k) * SLOT_UNITS + SLOT_UNITS)
                    sp.dma_start(adj_in[:, s],
                                 adj_t[:, bass.ds(k * SLOT_UNITS * UT, SLOT_UNITS * UT),
                                       bass.ds(g * GW, GW)]).then_inc(a_loaded[s], 16)

            def load_all_adj(g, par, more):
                with sp.Fori(0, LOADS // NSLOT // 2) as i:
                    load_adj(g, i)
                if more:
                    load_group(g + 1, 1 - par)
                with sp.Fori(LOADS // NSLOT // 2, LOADS // NSLOT) as i:
                    load_adj(g, i)

            load_group(0, 0)
            with sp.Fori(0, GROUPS // 2 - 1) as g2:
                load_all_adj(g2 * 2, 0, True)
                load_all_adj(g2 * 2 + 1, 1, True)
            load_all_adj(GROUPS - 2, 0, True)
            load_all_adj(GROUPS - 1, 1, False)

        @block.tensor
        def _(pe):
            pe.wait_ge(consts_ready, 1)
            pe.wait_ge(w_loaded, 16)
            nc.tensor.transpose(ps[:, 0, 0:P], w_nat[:, :], ident[:, :]).then_inc(wT_ready, 1)
            pe.wait_ge(att_loaded, 16 * 2 * HEADS)
            nc.tensor.matmul(ps[:, 1, 0:2 * HEADS], w_nat[:, :], att[:, :], start=True, stop=True).then_inc(wa_ready, 1)
            pe.wait_ge(wa_copied, 1)
            pe.wait_ge(wT_copied, 1)
            pe.wait_ge(x_loaded, 16 * XLOADS)

            def transpose_chunk(c):
                for j in range(CH):
                    t = c * CH + j
                    last = nc.tensor.transpose(ps[:, c % 2, j * P:(j + 1) * P], ring[:, t * FEAT:(t + 1) * FEAT], ident[:, :])
                last.then_inc(xT_ready, 1)

            def project_chunk(c):
                pe.wait_ge(xT_copied, c + 1)
                pe.wait_ge(h_free, c + 1)
                for j in range(CH):
                    last = nc.tensor.matmul(ps[:, 2 + 2 * (c % 2) + j // 2, (j % 2) * HCOLS:(j % 2 + 1) * HCOLS],
                                            xT[:, c % 2, j * P:(j + 1) * P], w_rhs[:, :], start=True, stop=True)
                last.then_inc(h_ready, 1)

            transpose_chunk(0)
            for c in range(TILES // CH):
                if c + 1 < TILES // CH:
                    transpose_chunk(c + 1)
                project_chunk(c)
            pe.wait_ge(h_free, TILES // CH + 2)
            pe.sem_inc(units_done, BODY)
            pe.wait_ge(dcol_ready, 1)
            dflat = dcol[:, :, :].rearrange("p h t -> p (h t)")
            for half in range(2):
                last = nc.tensor.transpose(ps[:, 6, half * P:(half + 1) * P],
                                           dflat[:, half * P:(half + 1) * P], ident[:, :])
            last.then_inc(dT_ready, 1)
            pe.wait_ge(dT_copied, 1)
            pe.wait_ge(lo_ready, TILES // VT + 2)
            pe.wait_ge(hi_ready, TILES // VT)

            with pe.Fori(0, GROUPS) as g:
                for b in range(BLKS):
                    pe.wait_ge(evac_act, BLKS * g + b + 1)
                    pe.wait_ge(evac_dve, BLKS * g + b + 1)
                    for k in range(2):
                        nc.tensor.matmul(ps[:, 2 * b + k, 0:1], zeros16[:, :], zeros16[:, 0:1],
                                         start=True, stop=False, skip_group_check=True)
                for u in range(UNITS):
                    q = u % NMASK
                    pe.wait_ge(masks_ready, g * UNITS + u + 1)
                    pe.sem_inc(pe_tick, 1)
                    for j in range(UT):
                        t = u * UT + j
                        heads = vals[:, t * TW:(t + 1) * TW].rearrange("p (h c) -> p h c", h=HEADS)
                        for b in range(BLKS):
                            m = slice(b * P, (b + 1) * P)
                            nc.tensor.matmul(ps[:, 2 * b, 0:PW].rearrange("p (h c) -> p h c", h=HEADS),
                                             adj16[:, u // SLOT_UNITS % NSLOT, u % SLOT_UNITS * UT + j, m], heads[:, :, HL:HW],
                                             start=False, stop=False, skip_group_check=True)
                            for h in range(HEADS):
                                o = ps[:, 2 * b, PW:PW + HW] if h == 0 else ps[:, 2 * b + 1, (h - 1) * HW:h * HW]
                                last = nc.tensor.matmul(o, mask8[:, q, j, h, m], heads[:, h, :],
                                                        start=False, stop=False, skip_group_check=True)
                    last.then_inc(units_done, 1)
                for b in range(BLKS):
                    for k in range(2):
                        last = nc.tensor.matmul(ps[:, 2 * b + k, 0:1], zeros16[:, :], zeros16[:, 0:1],
                                                start=False, stop=True, skip_group_check=True)
                last.then_inc(sums_done, 1)

        @block.scalar
        def _(act):
            act.wait_ge(att_zeroed, 1)
            for k, a in enumerate((att_src, att_dst)):
                for h in range(HEADS):
                    act.dma_start(att[h * FO:(h + 1) * FO, k * HEADS + h:k * HEADS + h + 1],
                                  a[0, h, :].unsqueeze(1)).then_inc(att_loaded, 16)
            with act.Fori(0, TILES // CH // 2) as i:
                for b in range(2):
                    act.wait_ge(xT_ready, i * 2 + b + 1)
                    act.wait_ge(h_free, i * 2 + b + 1)
                    nc.scalar.copy(xT[:, b, :], ps[:, b, :]).then_inc(xT_copied, 1)
            act.wait_ge(shifted, 1)
            sflat = sp_[:, :, :].rearrange("p t h -> p (t h)")
            nc.scalar.activation(e1[:, :], sflat, ACT.Exp)
            nc.scalar.activation(e2[:, :], sflat, ACT.Exp, scale=0.2)
            nc.scalar.activation(w_m[:, :], w_log[:, :], ACT.Exp, scale=0.8).then_inc(exps_ready, 1)
            with act.Fori(0, TILES // VT // 2) as i:
                for b in range(2):
                    c = i * 2 + b
                    v = vals[:, bass.ds(c * VT * TW, VT * TW)].rearrange("p (q s c) -> p q s c", s=2, c=HL)
                    for k, ready in ((0, f1_ready), (1, f2_ready)):
                        act.wait_ge(ready, c + 1)
                        last = nc.scalar.mul(v[:, :, k, 0:VW], fval[:, b, k, :].rearrange("p (q c) -> p q c", c=VW), 1.0 / SPLIT)
                    last.then_inc(hi_ready, 1)

            def signs(g, u0, u, par):
                q = u % NMASK
                act.wait_ge(units_done, g * UNITS + u0 + u + BODY - NMASK + 1)
                act.sem_inc(act_tick, 1)
                for j, h in act_pairs(u):
                    last = nc.scalar.activation(
                        flags[:, q, j, h, :], d_bc[:, bass.ds(par * (HEADS * GW) + h * GW, GW)],
                        ACT.Sigmoid, bias=big_s[:, bass.ds(((u0 + u) * UT + j) * HEADS + h, 1)], scale=STEEP)
                last.then_inc(signs_ready, 1)

            def evacuate(g):
                act.wait_ge(sums_free, g + 1)
                act.wait_ge(sums_done, g + 1)
                for b in range(BLKS):
                    nc.scalar.copy(sum_adj[:, b], ps[:, 2 * b, 0:PW].rearrange("p (h c) -> p h c", h=HEADS))
                    nc.scalar.copy(sum_head[:, b, 0], ps[:, 2 * b, PW:PW + HW]).then_inc(evac_act, 1)

            def first_units(g, par, before):
                act.wait_ge(d_loaded[0], 16 * ((g + 2) // 2))
                if before is not None:
                    act.wait_ge(d_loaded[1], 16 * ((g + 1) // 2))
                for u in range(BODY):
                    signs(g, 0, u, par)
                    if u == EVAC_ACT and before is not None:
                        evacuate(before)

            def other_units(g, par):
                with act.Fori(1, UNITS // BODY) as i:
                    u0 = i * BODY
                    for u in range(BODY):
                        signs(g, u0, u, par)
                act.drain().then_inc(d_read_act, 1)

            act.wait_ge(lo_ready, TILES // VT + 2)
            act.wait_ge(f2_ready, TILES // VT)
            act.sem_inc(d_read_act, 2)
            act.sem_inc(evac_act, BLKS)
            first_units(0, 0, None)
            with act.Fori(0, GROUPS - 1) as g:
                other_units(g, g % 2)
                first_units(g + 1, (g + 1) % 2, g)
            other_units(GROUPS - 1, (GROUPS - 1) % 2)
            evacuate(GROUPS - 1)

        @block.vector
        def _(dve):
            steps = [0]

            def link(ins):
                steps[0] += 1
                ins.then_inc(dve_step, 1)
                dve.wait_ge(dve_step, steps[0])

            nc.vector.memset(zeros16[:, :], 0.0)
            nc.vector.memset(att[:, :], 0.0).then_inc(att_zeroed, 1)
            dve.wait_ge(wT_ready, 1)
            nc.vector.tensor_copy(w_rhs[:, 0:HEADS * FO], ps[:, 0, 0:P]).then_inc(wT_copied, 1)
            dve.wait_ge(wa_ready, 1)
            nc.vector.tensor_copy(w_rhs[:, HEADS * FO:HCOLS], ps[:, 1, 0:2 * HEADS]).then_inc(wa_copied, 1)
            dve.sem_inc(h_free, 2)
            dve.wait_ge(bias_loaded, 16)
            with dve.Fori(0, TILES // CH // 2) as i:
                for b in range(2):
                    c = i * 2 + b
                    dve.wait_ge(h_ready, c + 1)
                    hc = hp[:, bass.ds(c * CH * HEADS * VW, CH * HEADS * VW)].rearrange("p (q v) -> p q v", v=VW)[:, :, 0:FO]
                    for k in range(2):
                        src = ps[:, 2 + 2 * b + k, 0:2 * HCOLS].rearrange("p (j c) -> p j c", j=2)
                        nc.vector.tensor_copy(sd[:, bass.ds(c * CH + 2 * k, 2), :], src[:, :, HEADS * FO:HCOLS])
                        last = nc.vector.tensor_tensor(
                            hc[:, 2 * k * HEADS:2 * (k + 1) * HEADS, :].rearrange("p (j h) v -> p j h v", h=HEADS),
                            src[:, :, 0:HEADS * FO].rearrange("p j (h v) -> p j h v", h=HEADS),
                            bias_bc[:, :].rearrange("p (h v) -> p h v", h=HEADS).unsqueeze(1)
                            .to_broadcast([P, 2, HEADS, FO]), ALU.add)
                    last.then_inc(h_free, 1)
                    dve.wait_ge(h_free, c + 3)
                    nc.vector.tensor_reduce(habs[:, bass.ds(c, 1)], hc, axis=AX.XY, op=ALU.max,
                                            apply_absolute_value=True).then_inc(habs_ready, 1)
            dve.wait_ge(habs_ready, TILES // CH)
            nc.vector.tensor_copy(dcol[:, :, :], sd[:, :, HEADS:2 * HEADS].rearrange("p t h -> p h t")).then_inc(dcol_ready, 1)
            nc.vector.tensor_reduce(mx[:, 0:HEADS], sd[:, :, 0:HEADS].rearrange("p t h -> p h t"), axis=AX.X, op=ALU.max)
            nc.vector.tensor_reduce(mx[:, HEADS:HEADS + 1], habs[:, :], axis=AX.X, op=ALU.max).then_inc(maxima_ready, 1)
            nc.vector.tensor_scalar(neg_s[:, :].rearrange("p (t h) -> p t h", h=HEADS), sd[:, :, 0:HEADS],
                                    -1.0, None, ALU.mult)
            nc.vector.tensor_scalar(big_s[:, :].rearrange("p (t h) -> p t h", h=HEADS), sd[:, :, 0:HEADS],
                                    STEEP, None, ALU.mult)
            dve.wait_ge(maxima_all, 1)
            smax = mxa[:, 0:HEADS].unsqueeze(1).to_broadcast([P, TILES, HEADS])
            nc.vector.tensor_tensor(sp_[:, :, :], sd[:, :, 0:HEADS], smax, ALU.subtract)
            nc.vector.tensor_tensor(w_log[:, :].rearrange("p (t h) -> p t h", h=HEADS), sd[:, :, HEADS:2 * HEADS],
                                    smax, ALU.add).then_inc(shifted, 1)
            link(nc.vector.tensor_scalar(hscale[:, :], mxa[:, HEADS:HEADS + 1], 1.0, None, ALU.max))
            link(nc.vector.reciprocal(hscale2[:, :], hscale[:, :]))
            link(nc.vector.tensor_scalar(hscale[:, :], hscale2[:, :], TOP * SPLIT, None, ALU.mult))
            dve.wait_ge(dT_ready, 1)
            nc.vector.tensor_copy(dT[:, :, :], ps[:, 6, 0:2 * P].rearrange("p (a b) -> p a b", a=2)).then_inc(dT_copied, 1)
            dve.wait_ge(exps_ready, 1)
            link(nc.vector.tensor_scalar(e1[:, :], e1[:, :], hscale[:, :], None, ALU.mult))
            nc.vector.tensor_scalar(e2[:, :], e2[:, :], hscale[:, :], None, ALU.mult).then_inc(exps_scaled, 1)
            for h in range(HEADS):
                wh = w_m[:, :].rearrange("p (t h) -> p t h", h=HEADS)[:, :, h]
                link(nc.vector.tensor_scalar(wh, wh, INV[h], None, ALU.mult))

            def product(i, b):
                c = i * 2 + b
                dve.wait_ge(lo_ready, c + 1)
                nc.vector.tensor_tensor(
                    fval[:, b, 0, :].rearrange("p (q c) -> p q c", c=VW),
                    hp[:, bass.ds(c * FV, FV)].rearrange("p (q c) -> p q c", c=VW),
                    e1[:, bass.ds(c * VT * HEADS, VT * HEADS)].unsqueeze(2).to_broadcast([P, VT * HEADS, VW]),
                    ALU.mult).then_inc(f1_ready, 1)

            def low_parts(i, b):
                c = i * 2 + b
                dve.wait_ge(hi_ready, c + 1)
                v = vals[:, bass.ds(c * VT * TW, VT * TW)].rearrange("p (q s c) -> p q s c", s=2, c=HL)
                for k in range(2):
                    last = nc.vector.scalar_tensor_tensor(v[:, :, k, VW:HL], v[:, :, k, 0:VW], -SPLIT,
                                                          fval[:, b, k, :].rearrange("p (q c) -> p q c", c=VW),
                                                          ALU.mult, ALU.add)
                last.then_inc(lo_ready, 1)

            dve.sem_inc(lo_ready, 2)
            product(0, 0)
            with dve.Fori(0, TILES // VT // 2 - 1) as i:
                product(i, 1)
                low_parts(i, 0)
                product(i + 1, 0)
                low_parts(i, 1)
            product(TILES // VT // 2 - 1, 1)
            low_parts(TILES // VT // 2 - 1, 0)
            low_parts(TILES // VT // 2 - 1, 1)
            dve.sem_inc(d_read_dve, 2)
            dve.sem_inc(evac_dve, BLKS)
            dve.sem_inc(sums_free, 1)
            dve.sem_inc(xres_free, 2)
            dve.sem_inc(y_free, 1)

            def compares(g, body, u):
                q = u % NMASK
                unit = body * BODY + u
                if u == 0 and isinstance(body, int) and body == 0:
                    dve.wait_ge(d_loaded[0], 16 * ((g + 2) // 2))
                    if not isinstance(g, int) or g > 0:
                        dve.wait_ge(d_loaded[1], 16 * ((g + 1) // 2))
                dve.wait_ge(units_done, g * UNITS + unit + BODY - NMASK + 1)
                for j, h in dve_pairs(u):
                    last = nc.vector.tensor_scalar(
                        flags[:, q, j, h, :], d_bc[:, bass.ds((g % 2) * (HEADS * GW) + h * GW, GW)],
                        neg_s[:, bass.ds((unit * UT + j) * HEADS + h, 1)], FLAG[h], ALU.is_gt, ALU.mult)
                last.then_inc(compares_done, 1)

            def combine_words(g, body, u):
                q, s = u % NMASK, u // SLOT_UNITS % NSLOT
                j0 = u % SLOT_UNITS * UT
                done = g * UNITS + body * BODY + u
                if u % SLOT_UNITS == 0:
                    dve.wait_ge(a_loaded[s], 16 * (g * (LOADS // NSLOT) + body + 1))
                dve.wait_ge(signs_ready, done + 1)
                dve.wait_ge(compares_done, done + 1)
                nc.vector.scalar_tensor_tensor(words[:, q], words[:, q], WORD, adj_in[:, s, j0:j0 + UT, :],
                                               ALU.mult, ALU.mult).then_inc(masks_ready, 1)

            def body_units(g, body, after, hooks={}):
                for u in range(BODY):
                    if u + 1 < BODY:
                        compares(g, body, u + 1)
                    elif after is not None:
                        compares(after[0], after[1], 0)
                    combine_words(g, body, u)
                    if u in hooks:
                        hooks[u]()

            def evacuate(g):
                dve.wait_ge(sums_free, g + 1)
                dve.wait_ge(sums_done, g + 1)
                for b in range(BLKS):
                    nc.vector.tensor_copy(sum_head[:, b, 1:HEADS], ps[:, 2 * b + 1, 0:3 * HW].rearrange("p (h c) -> p h c", h=3)
                                          ).then_inc(evac_dve, 1)

            CHAIN = 9
            chain = [0]

            def step(g, ins):
                chain[0] += 1
                ins.then_inc(final_step, 1)
                dve.wait_ge(final_step, g * CHAIN + chain[0])

            flat = dict(adj=sum_adj[:, :, :, :].rearrange("p b h c -> p (b h) c"),
                        head=sum_head[:, :, :, :].rearrange("p b h c -> p (b h) c"))

            def combine(g):
                chain[0] = 0
                dve.wait_ge(evac_act, BLKS * g + 2 * BLKS)
                dve.wait_ge(evac_dve, BLKS * g + 2 * BLKS)
                for h in range(HEADS):
                    last = nc.vector.scalar_tensor_tensor(sum_adj[:, :, h, :], sum_head[:, :, h, HL:HW], -INV[h],
                                                          sum_adj[:, :, h, :], ALU.mult, ALU.add)
                nc.vector.scalar_tensor_tensor(num1[:, :, :], flat["head"][:, :, VW:HL], 1.0 / SPLIT,
                                               flat["head"][:, :, 0:VW], ALU.mult, ALU.add)
                step(g, last)
                step(g, nc.vector.scalar_tensor_tensor(num[:, :, :], flat["adj"][:, :, VW:HL], 1.0 / SPLIT,
                                                       flat["adj"][:, :, 0:VW], ALU.mult, ALU.add))
                dve.sem_inc(sums_free, 1)

            def attend(g, par):
                w = w_m[:, bass.ds(g * (BLKS * HEADS), BLKS * HEADS)].unsqueeze(2).to_broadcast([P, BLKS * HEADS, VW])
                step(g, nc.vector.tensor_tensor(num1[:, :, :], num1[:, :, :], w, ALU.mult))
                step(g, nc.vector.tensor_tensor(num[:, :, :], num[:, :, :], num1[:, :, :], ALU.add))
                step(g, nc.vector.reciprocal(rden[:, :], num[:, :, FO]))
                dve.wait_ge(y_free, g + 1)
                yh = y[:, :, :].rearrange("p b (h v) -> p (b h) v", h=HEADS)
                step(g, nc.vector.tensor_tensor(yh, num[:, :, 0:FO],
                                                rden[:, :].unsqueeze(2).to_broadcast([P, BLKS * HEADS, FO]), ALU.mult))
                dve.wait_ge(xres_loaded[0], 16 * ((g + 2) // 2))
                if not isinstance(g, int) or g > 0:
                    dve.wait_ge(xres_loaded[1], 16 * ((g + 1) // 2))
                step(g, nc.vector.tensor_tensor(y[:, :, :].rearrange("p b f -> p (b f)"), y[:, :, :].rearrange("p b f -> p (b f)"),
                                                xres[:, bass.ds(par * (BLKS * FEAT), BLKS * FEAT)], ALU.add))
                dve.sem_inc(xres_free, 1)
                for b in range(BLKS):
                    last = nc.vector.bn_stats(stats[:, b, :], y[:, b, :])
                step(g, last)
                dve.sem_inc(dve_tick, 1)
                for b in range(BLKS):
                    last = nc.vector.bn_aggr(mv[:, b, :], stats[:, b, :])
                step(g, last)
                nc.vector.tensor_scalar(rstd[:, 0:BLKS], mv[:, :, 1], EPS, None, ALU.add).then_inc(var_ready, 1)
                assert chain[0] == CHAIN

            def normalize(g):
                dve.wait_ge(rstd_ready, g + 1)
                for b in range(BLKS):
                    last = nc.vector.tensor_scalar(y[:, b, :], y[:, b, :], mv[:, b, 0:1], rstd[:, b:b + 1],
                                                   ALU.subtract, ALU.mult)
                last.then_inc(y_ready, 1)

            def end_of(g):
                return {EVAC_DVE: lambda: evacuate(g), EVAC_DVE + 1: lambda: combine(g),
                        EVAC_DVE + 3: lambda: attend(g, g % 2), EVAC_DVE + 5: lambda: normalize(g)}

            def other_units(g, after):
                with dve.Fori(1, UNITS // BODY - 1) as i:
                    body_units(g, i, (g, i + 1))
                body_units(g, UNITS // BODY - 1, after)
                dve.wait_ge(masks_ready, g * UNITS + UNITS)
                dve.sem_inc(d_read_dve, 1)

            compares(0, 0, 0)
            body_units(0, 0, (0, 1))
            with dve.Fori(0, GROUPS - 1) as g:
                other_units(g, (g + 1, 0))
                body_units(g + 1, 0, (g + 1, 1), end_of(g))
            other_units(GROUPS - 1, None)
            evacuate(GROUPS - 1)
            combine(GROUPS - 1)
            attend(GROUPS - 1, (GROUPS - 1) % 2)
            normalize(GROUPS - 1)

        @block.gpsimd
        def _(pool):
            nc.gpsimd.memset(ident[:, :], 0.0).then_inc(pool_step, 1)
            pool.wait_ge(pool_step, 1)
            nc.gpsimd.affine_select(out=ident[:, :], in_=ident[:, :], compare_op=ALU.not_equal, fill=1.0, base=0,
                                    pattern=[[-1, P]], channel_multiplier=1).then_inc(consts_ready, 1)
            nc.gpsimd.memset(halfpow[:, :], -0.5)
            nc.gpsimd.memset(hp[:, :].rearrange("p (q v) -> p q v", v=VW)[:, :, FO:VW], 1.0)
            pool.wait_ge(maxima_ready, 1)
            nc.gpsimd.partition_all_reduce(mxa[:, :], mx[:, :], P, bass.bass_isa.ReduceOp.max).then_inc(maxima_all, 1)
            pool.wait_ge(exps_scaled, 1)
            with pool.Fori(0, TILES // VT // 2) as i:
                for b in range(2):
                    c = i * 2 + b
                    pool.wait_ge(lo_ready, c + 1)
                    nc.gpsimd.tensor_tensor(
                        fval[:, b, 1, :].rearrange("p (q c) -> p q c", c=VW),
                        hp[:, bass.ds(c * FV, FV)].rearrange("p (q c) -> p q c", c=VW),
                        e2[:, bass.ds(c * VT * HEADS, VT * HEADS)].unsqueeze(2).to_broadcast([P, VT * HEADS, VW]),
                        ALU.mult).then_inc(f2_ready, 1)
            with pool.Fori(0, GROUPS) as g:
                pool.wait_ge(var_ready, g + 1)
                nc.gpsimd.tensor_tensor(rstd[:, :], rstd[:, :], halfpow[:, :], ALU.pow).then_inc(rstd_ready, 1)
                pool.wait_ge(y_ready, g + 1)
                pool.sem_inc(pool_tick, 1)
                pool.dma_start(out_t[:, bass.ds(g * BLKS, BLKS), :], y[:, :, :]).then_inc(out_stored, 16)
                pool.wait_ge(out_stored, 16 * g + 16)
                pool.sem_inc(y_free, 1)


_INS = ["x", "adj", "L0_gnn_weight", "L0_gnn_att_src", "L0_gnn_att_dst", "L0_gnn_bias"]


def kernel(**inputs):
    import numpy as np
    import concourse.bacc as bacc
    from concourse.bass_utils import run_bass_kernel_spmd

    nc = bacc.Bacc("TRN2", target_bir_lowering=False, num_devices=1)
    arrays, args = {}, []
    for name in _INS:
        a = np.ascontiguousarray(inputs[name])
        arrays[f"in_{name}"] = a
        args.append(nc.dram_tensor(f"in_{name}", a.shape, mybir.dt.from_np(a.dtype), kind="ExternalInput").ap())
    shape = arrays["in_x"].shape
    args.append(nc.dram_tensor("out", shape, mybir.dt.from_np(np.dtype("float32")), kind="ExternalOutput").ap())
    gat_residual_layernorm(nc, *args)
    r = run_bass_kernel_spmd(nc, [arrays], core_ids=[0])
    return r.results[0]["out"]
```

```python
import concourse.bass as bass
from concourse import mybir
from contextlib import ExitStack

F32 = mybir.dt.float32
F16 = mybir.dt.float16
F8 = mybir.dt.float8e4
U8 = mybir.dt.uint8
BF16 = mybir.dt.bfloat16
I32 = mybir.dt.int32
ALU = mybir.AluOpType
ACT = mybir.ActivationFunctionType
AX = mybir.AxisListType


def gat_residual_layernorm(nc, x, adj, weight, att_src, att_dst, bias, out):
    P = 128
    N, FEAT = x.shape
    HEADS, FO = att_src.shape[1], att_src.shape[2]
    TILES = N // P
    GW = 512
    GROUPS = N // GW
    BLKS = GW // P
    UT = 2
    UNITS = TILES // UT
    SLOT_UNITS = 2
    LOADS = UNITS // SLOT_UNITS
    NSLOT = 4
    NMASK = 8
    BODY = NSLOT * SLOT_UNITS
    VW = FO + 1
    HL = 2 * VW
    HW = 2 * HL
    TW = HEADS * HW
    PW = HEADS * HL
    BANK = 512
    FLAG = [2.0, 1.0, 1.0, 1.0]
    WORD = 32.0
    INV = [0.5, 8.0, 8.0, 8.0]
    STEEP = 2.0 ** 40
    SPLIT = 2.0 ** 11
    TOP = 2.0 ** 14
    EPS = 1e-5
    EVACUATE = 3
    DVE_FOUR = (0, 2, 4, 5, 6, 7)
    FIRST_FOUR = (1,)
    HCOLS = HEADS * FO + 2 * HEADS
    XLOADS = 4
    CH = 4
    VT = 4
    def dve_pairs(u, ends_last):
        return [(0, 0), (1, 0), (0, 1)] + ([(1, 1)] if u in (FIRST_FOUR if ends_last else DVE_FOUR) else [])

    def act_pairs(u, ends_last):
        return [(j, h) for j in range(UT) for h in range(HEADS) if (j, h) not in dve_pairs(u, ends_last)]

    x_t = x.rearrange("(t p) f -> p t f", p=P)
    out_t = out.rearrange("(t p) f -> p t f", p=P)
    adj_t = adj.rearrange("(t p) m -> p t m", p=P)
    d_rows = nc.dram_tensor("d_rows", (HEADS, N), F32, kind="Internal").ap()

    ctx = ExitStack()
    with ctx:
        def sb(name, shape, dt):
            return ctx.enter_context(nc.sbuf_tensor(name, shape, dt))

        def sem(name):
            return ctx.enter_context(nc.semaphore(name))

        vals = sb("vals", [P, TILES * TW], F16)
        SLOT = SLOT_UNITS * UT * GW
        ring = sb("ring", [P, NSLOT * SLOT], F32)
        adj_in = ring[:, :].rearrange("p (s j m) -> p s j m", s=NSLOT, m=GW)
        hp = sb("hp", [P, TILES * HEADS * VW], F32)
        mask = hp[:, 0:NMASK * UT * GW]
        words = mask.bitcast(I32).rearrange("p (q j m) -> p q j m", q=NMASK, j=UT)
        flags = mask.bitcast(U8).rearrange("p (q j m h) -> p q j h m", q=NMASK, j=UT, h=HEADS)
        mask8 = mask.bitcast(F8).rearrange("p (q j m h) -> p q j h m", q=NMASK, j=UT, h=HEADS)
        adj16 = ring[:, :].bitcast(BF16).rearrange("p (s j m two) -> p s j m two", s=NSLOT, m=GW, two=2)[:, :, :, :, 1]
        d_bc = sb("d_bc", [P, 2 * HEADS * GW], F32)
        SUMS = 3 * HEADS
        sums_raw = sb("sums_raw", [P, BLKS * 2, SUMS // 2, HL], F32)
        sums = sb("sums", [P, BLKS, SUMS, VW], F32)
        num = sb("num", [P, BLKS, HEADS, VW], F32)
        num1 = sb("num1", [P, BLKS, HEADS, VW], F32)
        rden = sb("rden", [P, BLKS * HEADS], F32)
        xres = sb("xres", [P, 2 * BLKS * FEAT], F32)
        y = sb("y", [P, BLKS, FEAT], F32)
        stats = sb("stats", [P, BLKS, 6], F32)
        mv = sb("mv", [P, BLKS, 2], F32)
        rstd = sb("rstd", [P, BLKS], F32)
        halfpow = sb("halfpow", [P, BLKS], F32)
        bias_bc = sb("bias_bc", [P, FEAT], F32)
        sd = sb("sd", [P, TILES, 2 * HEADS], F32)
        big_s = sb("big_s", [P, TILES * HEADS], F32)
        neg_s = sb("neg_s", [P, TILES * HEADS], F32)
        w_log = sb("w_log", [P, TILES * HEADS], F32)
        w_m = sb("w_m", [P, TILES * HEADS], F32)
        e1 = sb("e1", [P, TILES * HEADS], F32)
        e2 = sb("e2", [P, TILES * HEADS], F32)
        s_shift = sb("s_shift", [P, TILES, HEADS], F32)
        dcol = sb("dcol", [P, HEADS, TILES], F32)
        dT = sb("dT", [P, 2, P], F32)
        habs = sb("habs", [P, TILES // CH], F32)
        mx = sb("mx", [P, HEADS + 1], F32)
        mxa = sb("mxa", [P, HEADS + 1], F32)
        hscale = sb("hscale", [P, 1], F32)
        hscale2 = sb("hscale2", [P, 1], F32)
        ident = sb("ident", [P, P], F32)
        warm = sb("warm", [P, 2], F32)
        zeros16 = sb("zeros16", [P, P], F16)
        w_nat = sb("w_nat", [P, FEAT], F32)
        att = sb("att", [P, 2 * HEADS], F32)
        w_rhs = sb("w_rhs", [P, HCOLS], F32)
        FV = VT * HEADS * VW
        NF = 4
        fbuf = sb("fbuf", [P, NF * 2 * FV], F32)
        fval = fbuf[:, :].rearrange("p (b k c) -> p b k c", b=NF, k=2)
        xT = fbuf[:, 0:2 * CH * P].rearrange("p (b n) -> p b n", b=2)

        ps = ctx.enter_context(nc.psum_tensor("ps", [P, 8, BANK], F32))

        w_loaded = sem("w_loaded")
        att_loaded = sem("att_loaded")
        att_issued = sem("att_issued")
        bias_loaded = sem("bias_loaded")
        x_loaded = [sem(f"x_loaded{i}") for i in range(XLOADS)]
        a_loaded = [sem(f"a_loaded{i}") for i in range(NSLOT)]
        d_loaded = [sem(f"d_loaded{i}") for i in range(2)]
        xres_loaded = [sem(f"xres_loaded{i}") for i in range(2)]
        d_stored = sem("d_stored")
        out_stored = sem("out_stored")
        att_zeroed = sem("att_zeroed")
        consts_ready = sem("consts_ready")
        wT_ready = sem("wT_ready")
        wT_copied = sem("wT_copied")
        wa_ready = sem("wa_ready")
        wa_copied = sem("wa_copied")
        xT_ready = sem("xT_ready")
        xT_copied = sem("xT_copied")
        h_ready = sem("h_ready")
        h_free = sem("h_free")
        habs_ready = sem("habs_ready")
        dve_step = sem("dve_step")
        maxima_ready = sem("maxima_ready")
        maxima_all = sem("maxima_all")
        shifted = sem("shifted")
        exps_ready = sem("exps_ready")
        exps_scaled = sem("exps_scaled")
        dcol_ready = sem("dcol_ready")
        dT_ready = sem("dT_ready")
        dT_copied = sem("dT_copied")
        f1_ready = sem("f1_ready")
        f2_ready = sem("f2_ready")
        hi_ready = sem("hi_ready")
        lo_ready = sem("lo_ready")
        compares_done = sem("compares_done")
        signs_ready = sem("signs_ready")
        masks_ready = sem("masks_ready")
        units_done = sem("units_done")
        sums_done = sem("sums_done")
        sums_out = sem("sums_out")
        sums_free = sem("sums_free")
        xres_free = sem("xres_free")
        var_ready = sem("var_ready")
        rstd_ready = sem("rstd_ready")
        y_ready = sem("y_ready")
        y_free = sem("y_free")
        final_step = sem("final_step")
        pool_step = sem("pool_step")
        act_tick = sem("act_tick")
        dve_tick = sem("dve_tick")
        pe_tick = sem("pe_tick")
        pool_tick = sem("pool_tick")

        block = ctx.enter_context(nc.Block())

        @block.sync
        def _(sp):
            sp.dma_start(w_nat[:, :], weight).then_inc(w_loaded, 16)
            sp.dma_start(bias_bc[:, :], bias.partition_broadcast(P)).then_inc(bias_loaded, 16)
            sp.wait_ge(att_issued, 1)
            for k in range(XLOADS):
                t = TILES // XLOADS
                sp.dma_start(ring[:, k * t * FEAT:(k + 1) * t * FEAT].rearrange("p (t f) -> p t f", f=FEAT),
                             x_t[:, k * t:(k + 1) * t, :]).then_inc(x_loaded[k], 16)
            sp.wait_ge(dT_copied, 1)
            for half in range(2):
                rows = d_rows.rearrange("h (t p) -> (h t) p", p=P)[half * P:(half + 1) * P, :]
                sp.dma_start(rows, dT[:, half, :]).then_inc(d_stored, 16)
            sp.wait_ge(d_stored, 32)

            def load_group(g, par):
                sp.dma_start(d_bc[:, par * HEADS * GW:(par + 1) * HEADS * GW].rearrange("p (h m) -> p h m", h=HEADS),
                             d_rows[:, bass.ds(g * GW, GW)].partition_broadcast(P)).then_inc(d_loaded[par], 16)
                sp.wait_ge(xres_free, g + 1)
                sp.dma_start(xres[:, par * BLKS * FEAT:(par + 1) * BLKS * FEAT].rearrange("p (b f) -> p b f", b=BLKS),
                             x_t[:, bass.ds(g * BLKS, BLKS), :]).then_inc(xres_loaded[par], 16)

            def load_adj(g, i):
                for s in range(NSLOT):
                    k = i * NSLOT + s
                    sp.wait_ge(units_done, (g * LOADS + k) * SLOT_UNITS + SLOT_UNITS)
                    sp.dma_start(adj_in[:, s],
                                 adj_t[:, bass.ds(k * SLOT_UNITS * UT, SLOT_UNITS * UT),
                                       bass.ds(g * GW, GW)]).then_inc(a_loaded[s], 16)

            def load_all_adj(g, par, more):
                with sp.Fori(0, LOADS // NSLOT // 2) as i:
                    load_adj(g, i)
                if more:
                    load_group(g + 1, 1 - par)
                with sp.Fori(LOADS // NSLOT // 2, LOADS // NSLOT) as i:
                    load_adj(g, i)

            load_group(0, 0)
            with sp.Fori(0, GROUPS // 2 - 1) as g2:
                load_all_adj(g2 * 2, 0, True)
                load_all_adj(g2 * 2 + 1, 1, True)
            load_all_adj(GROUPS - 2, 0, True)
            load_all_adj(GROUPS - 1, 1, False)

        @block.tensor
        def _(pe):
            pe.wait_ge(consts_ready, 1)
            pe.wait_ge(w_loaded, 16)
            nc.tensor.transpose(ps[:, 0, 0:P], w_nat[:, :], ident[:, :]).then_inc(wT_ready, 1)
            pe.wait_ge(att_loaded, 16 * 2 * HEADS)
            nc.tensor.matmul(ps[:, 1, 0:2 * HEADS], w_nat[:, :], att[:, :], start=True, stop=True).then_inc(wa_ready, 1)
            pe.wait_ge(wa_copied, 1)
            pe.wait_ge(wT_copied, 1)

            def transpose_chunk(c):
                per_load = TILES // CH // XLOADS
                if c % per_load == 0:
                    pe.wait_ge(x_loaded[c // per_load], 16)
                for j in range(CH):
                    t = c * CH + j
                    last = nc.tensor.transpose(ps[:, c % 2, j * P:(j + 1) * P], ring[:, t * FEAT:(t + 1) * FEAT], ident[:, :])
                last.then_inc(xT_ready, 1)

            def project_chunk(c):
                pe.wait_ge(xT_copied, c + 1)
                pe.wait_ge(h_free, c + 1)
                for j in range(CH):
                    last = nc.tensor.matmul(ps[:, 2 + 2 * (c % 2) + j // 2, (j % 2) * HCOLS:(j % 2 + 1) * HCOLS],
                                            xT[:, c % 2, j * P:(j + 1) * P], w_rhs[:, :], start=True, stop=True)
                last.then_inc(h_ready, 1)

            transpose_chunk(0)
            for c in range(TILES // CH):
                if c + 1 < TILES // CH:
                    transpose_chunk(c + 1)
                project_chunk(c)
            pe.wait_ge(h_free, TILES // CH + 2)
            pe.sem_inc(units_done, BODY)
            pe.wait_ge(dcol_ready, 1)
            dflat = dcol[:, :, :].rearrange("p h t -> p (h t)")
            for half in range(2):
                last = nc.tensor.transpose(ps[:, 6, half * P:(half + 1) * P],
                                           dflat[:, half * P:(half + 1) * P], ident[:, :])
            last.then_inc(dT_ready, 1)
            pe.wait_ge(dT_copied, 1)
            pe.wait_ge(lo_ready, TILES // VT + NF)
            pe.wait_ge(hi_ready, TILES // VT)

            def open_block(g, b):
                pe.wait_ge(sums_out, BLKS * g + b + 1)
                for k in range(2):
                    nc.tensor.matmul(ps[:, 2 * b + k, 0:1], zeros16[:, :], zeros16[:, 0:1],
                                     start=True, stop=False, skip_group_check=True)

            def close_block(b):
                for k in range(2):
                    last = nc.tensor.matmul(ps[:, 2 * b + k, 0:1], zeros16[:, :], zeros16[:, 0:1],
                                            start=False, stop=True, skip_group_check=True)
                last.then_inc(sums_done, 1)

            def products(u, b):
                m = slice(b * P, (b + 1) * P)
                for j in range(UT):
                    t = u * UT + j
                    heads = vals[:, t * TW:(t + 1) * TW].rearrange("p (h c) -> p h c", h=HEADS)
                    nc.tensor.matmul(ps[:, 2 * b, 0:PW].rearrange("p (h c) -> p h c", h=HEADS),
                                     adj16[:, u // SLOT_UNITS % NSLOT, u % SLOT_UNITS * UT + j, m], heads[:, :, HL:HW],
                                     start=False, stop=False, skip_group_check=True)
                    for h in range(HEADS):
                        o = ps[:, 2 * b, PW:PW + HW] if h == 0 else ps[:, 2 * b + 1, (h - 1) * HW:h * HW]
                        last = nc.tensor.matmul(o, mask8[:, u % NMASK, j, h, m], heads[:, h, :],
                                                start=False, stop=False, skip_group_check=True)
                return last

            with pe.Fori(0, GROUPS) as g:
                for u in range(UNITS - 2):
                    pe.wait_ge(masks_ready, g * UNITS + u + 1)
                    pe.sem_inc(pe_tick, 1)
                    for b in range(BLKS):
                        if u == 0:
                            open_block(g, b)
                        last = products(u, b)
                    last.then_inc(units_done, 1)
                pe.wait_ge(masks_ready, g * UNITS + UNITS)
                pe.sem_inc(pe_tick, 1)
                for b in range(BLKS):
                    for u in (UNITS - 2, UNITS - 1):
                        last = products(u, b)
                        if b == BLKS - 1:
                            last.then_inc(units_done, 1)
                    close_block(b)

        @block.scalar
        def _(act):
            act.wait_ge(att_zeroed, 1)
            for k, a in enumerate((att_src, att_dst)):
                for h in range(HEADS):
                    act.dma_start(att[h * FO:(h + 1) * FO, k * HEADS + h:k * HEADS + h + 1],
                                  a[0, h, :].unsqueeze(1)).then_inc(att_loaded, 16)
            act.sem_inc(att_issued, 1)
            act.wait_ge(consts_ready, 1)
            nc.scalar.activation(warm[:, 0:1], ident[:, 0:1], ACT.Exp)
            with act.Fori(0, TILES // CH // 2) as i:
                for b in range(2):
                    act.wait_ge(xT_ready, i * 2 + b + 1)
                    act.wait_ge(h_free, i * 2 + b + 1)
                    nc.scalar.copy(xT[:, b, :], ps[:, b, :]).then_inc(xT_copied, 1)
            act.wait_ge(shifted, 1)
            sflat = s_shift[:, :, :].rearrange("p t h -> p (t h)")
            nc.scalar.activation(e1[:, :], sflat, ACT.Exp)
            nc.scalar.activation(e2[:, :], sflat, ACT.Exp, scale=0.2)
            nc.scalar.activation(w_m[:, :], w_log[:, :], ACT.Exp, scale=0.8).then_inc(exps_ready, 1)
            nc.scalar.activation(warm[:, 1:2], ident[:, 0:1], ACT.Sigmoid)
            with act.Fori(0, TILES // VT // NF) as i:
                for b in range(NF):
                    c = i * NF + b
                    v = vals[:, bass.ds(c * VT * TW, VT * TW)].rearrange("p (q s c) -> p q s c", s=2, c=HL)
                    for k, ready in ((0, f1_ready), (1, f2_ready)):
                        act.wait_ge(ready, c + 1)
                        last = nc.scalar.mul(v[:, :, k, 0:VW], fval[:, b, k, :].rearrange("p (q c) -> p q c", c=VW), 1.0 / SPLIT)
                    last.then_inc(hi_ready, 1)

            def signs(g, u0, u, par, ends_last=False):
                q = u % NMASK
                act.wait_ge(units_done, g * UNITS + u0 + u + BODY - NMASK + 1)
                act.sem_inc(act_tick, 1)
                for j, h in act_pairs(u, ends_last):
                    last = nc.scalar.activation(
                        flags[:, q, j, h, :], d_bc[:, bass.ds(par * (HEADS * GW) + h * GW, GW)],
                        ACT.Sigmoid, bias=big_s[:, bass.ds(((u0 + u) * UT + j) * HEADS + h, 1)], scale=STEEP)
                last.then_inc(signs_ready, 1)

            def evacuate(g):
                act.wait_ge(sums_free, g + 1)
                for b in range(BLKS):
                    act.wait_ge(sums_done, g * BLKS + b + 1)
                    act.sem_inc(act_tick, 1)
                    for k in range(2 * b, 2 * b + 2):
                        last = nc.scalar.copy(sums_raw[:, k], ps[:, k, 0:SUMS // 2 * HL].rearrange("p (k c) -> p k c", c=HL))
                    last.then_inc(sums_out, 1)

            def first_units(g, par, before):
                act.wait_ge(d_loaded[0], 16 * ((g + 2) // 2))
                if before is not None:
                    act.wait_ge(d_loaded[1], 16 * ((g + 1) // 2))
                for u in range(BODY):
                    if before is None:
                        act.wait_ge(lo_ready, NF + min(TILES // VT, (u + 1) * UT * GW // FV + 1))
                    signs(g, 0, u, par, before is not None)
                    if u == EVACUATE and before is not None:
                        evacuate(before)

            def other_units(g, par):
                with act.Fori(1, UNITS // BODY) as i:
                    u0 = i * BODY
                    for u in range(BODY):
                        signs(g, u0, u, par)

            act.sem_inc(sums_out, BLKS)
            first_units(0, 0, None)
            with act.Fori(0, GROUPS - 1) as g:
                other_units(g, g % 2)
                first_units(g + 1, (g + 1) % 2, g)
            other_units(GROUPS - 1, (GROUPS - 1) % 2)
            evacuate(GROUPS - 1)

        @block.vector
        def _(dve):
            steps = [0]

            def link(ins):
                steps[0] += 1
                ins.then_inc(dve_step, 1)
                dve.wait_ge(dve_step, steps[0])

            nc.vector.memset(zeros16[:, :], 0.0)
            nc.vector.memset(att[:, :], 0.0).then_inc(att_zeroed, 1)
            dve.wait_ge(wT_ready, 1)
            nc.vector.tensor_copy(w_rhs[:, 0:HEADS * FO], ps[:, 0, 0:P]).then_inc(wT_copied, 1)
            dve.wait_ge(wa_ready, 1)
            nc.vector.tensor_copy(w_rhs[:, HEADS * FO:HCOLS], ps[:, 1, 0:2 * HEADS]).then_inc(wa_copied, 1)
            dve.sem_inc(h_free, 2)
            dve.sem_inc(xres_free, 2)
            dve.wait_ge(bias_loaded, 16)

            def h_of(c):
                return hp[:, bass.ds(c * CH * HEADS * VW, CH * HEADS * VW)].rearrange("p (q v) -> p q v", v=VW)[:, :, 0:FO]

            def take_chunk(i, b):
                c = i * 2 + b
                dve.wait_ge(h_ready, c + 1)
                for k in range(2):
                    src = ps[:, 2 + 2 * b + k, 0:2 * HCOLS].rearrange("p (j c) -> p j c", j=2)
                    nc.vector.tensor_copy(sd[:, bass.ds(c * CH + 2 * k, 2), :], src[:, :, HEADS * FO:HCOLS])
                    last = nc.vector.tensor_tensor(
                        h_of(c)[:, 2 * k * HEADS:2 * (k + 1) * HEADS, :].rearrange("p (j h) v -> p j h v", h=HEADS),
                        src[:, :, 0:HEADS * FO].rearrange("p j (h v) -> p j h v", h=HEADS),
                        bias_bc[:, :].rearrange("p (h v) -> p h v", h=HEADS).unsqueeze(1)
                        .to_broadcast([P, 2, HEADS, FO]), ALU.add)
                last.then_inc(h_free, 1)

            def largest(i, b):
                c = i * 2 + b
                dve.wait_ge(h_free, c + 3)
                nc.vector.tensor_reduce(habs[:, bass.ds(c, 1)], h_of(c), axis=AX.XY, op=ALU.max,
                                        apply_absolute_value=True).then_inc(habs_ready, 1)

            take_chunk(0, 0)
            with dve.Fori(0, TILES // CH // 2 - 1) as i:
                take_chunk(i, 1)
                largest(i, 0)
                take_chunk(i + 1, 0)
                largest(i, 1)
            take_chunk(TILES // CH // 2 - 1, 1)
            largest(TILES // CH // 2 - 1, 0)
            largest(TILES // CH // 2 - 1, 1)
            dve.wait_ge(habs_ready, TILES // CH)
            nc.vector.tensor_copy(dcol[:, :, :], sd[:, :, HEADS:2 * HEADS].rearrange("p t h -> p h t")).then_inc(dcol_ready, 1)
            nc.vector.tensor_reduce(mx[:, 0:HEADS], sd[:, :, 0:HEADS].rearrange("p t h -> p h t"), axis=AX.X, op=ALU.max)
            nc.vector.tensor_reduce(mx[:, HEADS:HEADS + 1], habs[:, :], axis=AX.X, op=ALU.max).then_inc(maxima_ready, 1)
            nc.vector.tensor_scalar(neg_s[:, :].rearrange("p (t h) -> p t h", h=HEADS), sd[:, :, 0:HEADS],
                                    -1.0, None, ALU.mult)
            nc.vector.tensor_scalar(big_s[:, :].rearrange("p (t h) -> p t h", h=HEADS), sd[:, :, 0:HEADS],
                                    STEEP, None, ALU.mult)
            dve.wait_ge(maxima_all, 1)
            smax = mxa[:, 0:HEADS].unsqueeze(1).to_broadcast([P, TILES, HEADS])
            nc.vector.tensor_tensor(s_shift[:, :, :], sd[:, :, 0:HEADS], smax, ALU.subtract)
            nc.vector.tensor_tensor(w_log[:, :].rearrange("p (t h) -> p t h", h=HEADS), sd[:, :, HEADS:2 * HEADS],
                                    smax, ALU.add).then_inc(shifted, 1)
            link(nc.vector.tensor_scalar(hscale[:, :], mxa[:, HEADS:HEADS + 1], 1.0, None, ALU.max))
            link(nc.vector.reciprocal(hscale2[:, :], hscale[:, :]))
            link(nc.vector.tensor_scalar(hscale[:, :], hscale2[:, :], TOP * SPLIT, None, ALU.mult))
            dve.wait_ge(dT_ready, 1)
            nc.vector.tensor_copy(dT[:, :, :], ps[:, 6, 0:2 * P].rearrange("p (a b) -> p a b", a=2)).then_inc(dT_copied, 1)
            dve.wait_ge(exps_ready, 1)
            link(nc.vector.tensor_scalar(e1[:, :], e1[:, :], hscale[:, :], None, ALU.mult))
            nc.vector.tensor_scalar(e2[:, :], e2[:, :], hscale[:, :], None, ALU.mult).then_inc(exps_scaled, 1)
            for h in range(HEADS):
                wh = w_m[:, :].rearrange("p (t h) -> p t h", h=HEADS)[:, :, h]
                last = nc.vector.tensor_scalar(wh, wh, INV[h], None, ALU.mult)
            link(last)

            def product(i, b):
                c = i * NF + b
                dve.wait_ge(lo_ready, c + 1)
                nc.vector.tensor_tensor(
                    fval[:, b, 0, :].rearrange("p (q c) -> p q c", c=VW),
                    hp[:, bass.ds(c * FV, FV)].rearrange("p (q c) -> p q c", c=VW),
                    e1[:, bass.ds(c * VT * HEADS, VT * HEADS)].unsqueeze(2).to_broadcast([P, VT * HEADS, VW]),
                    ALU.mult).then_inc(f1_ready, 1)

            def low_parts(i, b):
                c = i * NF + b
                dve.wait_ge(hi_ready, c + 1)
                v = vals[:, bass.ds(c * VT * TW, VT * TW)].rearrange("p (q s c) -> p q s c", s=2, c=HL)
                for k in range(2):
                    last = nc.vector.scalar_tensor_tensor(v[:, :, k, VW:HL], v[:, :, k, 0:VW], -SPLIT,
                                                          fval[:, b, k, :].rearrange("p (q c) -> p q c", c=VW),
                                                          ALU.mult, ALU.add)
                last.then_inc(lo_ready, 1)

            LEAD = 2
            dve.sem_inc(lo_ready, NF)
            for b in range(LEAD):
                product(0, b)
            with dve.Fori(0, TILES // VT // NF - 1) as i:
                for b in range(NF):
                    product(i + (b + LEAD) // NF, (b + LEAD) % NF)
                    low_parts(i, b)
            last_i = TILES // VT // NF - 1
            for b in range(NF):
                if b + LEAD < NF:
                    product(last_i, b + LEAD)
                low_parts(last_i, b)
            dve.sem_inc(sums_free, 1)
            dve.sem_inc(y_free, 1)

            def compares(g, body, u, ended=None, at=None):
                q = u % NMASK
                unit = body * BODY + u
                start = isinstance(body, int) and body == 0
                ends_last = start and not (isinstance(g, int) and g == 0)
                if u == 0 and start:
                    dve.wait_ge(d_loaded[0], 16 * ((g + 2) // 2))
                    if not isinstance(g, int) or g > 0:
                        dve.wait_ge(d_loaded[1], 16 * ((g + 1) // 2))
                dve.wait_ge(units_done, g * UNITS + unit + BODY - NMASK + 1)
                for n, (j, h) in enumerate(dve_pairs(u, ends_last)):
                    if n == 2 and ended is not None:
                        end_at(ended, at, "compares")
                    last = nc.vector.tensor_scalar(
                        flags[:, q, j, h, :], d_bc[:, bass.ds((g % 2) * (HEADS * GW) + h * GW, GW)],
                        neg_s[:, bass.ds((unit * UT + j) * HEADS + h, 1)], FLAG[h], ALU.is_gt, ALU.mult)
                last.then_inc(compares_done, 1)

            def combine_words(g, body, u):
                q, s = u % NMASK, u // SLOT_UNITS % NSLOT
                j0 = u % SLOT_UNITS * UT
                done = g * UNITS + body * BODY + u
                if u % SLOT_UNITS == 0:
                    dve.wait_ge(a_loaded[s], 16 * (g * (LOADS // NSLOT) + body + 1))
                dve.wait_ge(signs_ready, done + 1)
                dve.wait_ge(compares_done, done + 1)
                nc.vector.scalar_tensor_tensor(words[:, q], words[:, q], WORD, adj_in[:, s, j0:j0 + UT, :],
                                               ALU.mult, ALU.mult).then_inc(masks_ready, 1)

            def body_units(g, body, after, ended=None):
                for u in range(BODY):
                    if u + 1 < BODY:
                        compares(g, body, u + 1, ended, u)
                    elif after is not None:
                        compares(after[0], after[1], 0, ended, u)
                    end_at(ended, u, "words")
                    combine_words(g, body, u)
                    end_at(ended, u, "end")

            raw = sums_raw[:, :, :, :].rearrange("p q k c -> p (q k) c")
            masked = sums[:, :, HEADS:SUMS, :].rearrange("p b (h s) v -> p b h s v", s=2)
            quot = num[:, :, :, :].rearrange("p b h v -> p (b h) v")
            yh = y[:, :, :].rearrange("p b (h v) -> p (b h) v", h=HEADS)
            yf = y[:, :, :].rearrange("p b f -> p (b f)")

            def end_add_parts(g):
                dve.wait_ge(sums_out, BLKS * g + 2 * BLKS)
                nc.vector.scalar_tensor_tensor(sums[:, :, :, :].rearrange("p b k v -> p (b k) v"), raw[:, :, VW:HL],
                                               1.0 / SPLIT, raw[:, :, 0:VW], ALU.mult, ALU.add).then_inc(final_step, 1)

            def end_weigh(g):
                dve.wait_ge(final_step, g * STEPS + 1)
                dve.sem_inc(sums_free, 1)
                w = w_m[:, bass.ds(g * (BLKS * HEADS), BLKS * HEADS)].rearrange("p (b h) -> p b h", h=HEADS)
                nc.vector.scalar_tensor_tensor(num[:, :, 0, :], masked[:, :, 0, 1, :], -INV[0], sums[:, :, 0, :], ALU.mult, ALU.add)
                for b in range(BLKS):
                    nc.vector.scalar_tensor_tensor(num[:, b, 1:HEADS, :], masked[:, b, 1:HEADS, 1, :], -INV[1],
                                                   sums[:, b, 1:HEADS, :], ALU.mult, ALU.add)
                nc.vector.tensor_tensor(num1[:, :, :, :], masked[:, :, :, 0, :],
                                        w.unsqueeze(3).to_broadcast([P, BLKS, HEADS, VW]), ALU.mult).then_inc(final_step, 1)

            def end_add(g):
                dve.wait_ge(final_step, g * STEPS + 2)
                nc.vector.tensor_tensor(num[:, :, :, :], num[:, :, :, :], num1[:, :, :, :], ALU.add).then_inc(final_step, 1)

            def end_reciprocal(g):
                dve.wait_ge(final_step, g * STEPS + 3)
                nc.vector.reciprocal(rden[:, :], quot[:, :, FO]).then_inc(final_step, 1)

            def end_divide(g):
                dve.wait_ge(final_step, g * STEPS + 4)
                dve.wait_ge(y_free, g + 1)
                nc.vector.tensor_tensor(yh, quot[:, :, 0:FO], rden[:, :].unsqueeze(2).to_broadcast([P, BLKS * HEADS, FO]),
                                        ALU.mult).then_inc(final_step, 1)

            def end_residual(g):
                dve.wait_ge(final_step, g * STEPS + 5)
                dve.wait_ge(xres_loaded[0], 16 * ((g + 2) // 2))
                if not isinstance(g, int) or g > 0:
                    dve.wait_ge(xres_loaded[1], 16 * ((g + 1) // 2))
                nc.vector.tensor_tensor(yf, yf, xres[:, bass.ds((g % 2) * (BLKS * FEAT), BLKS * FEAT)], ALU.add
                                        ).then_inc(final_step, 1)

            def end_moments(g):
                dve.wait_ge(final_step, g * STEPS + 6)
                dve.sem_inc(xres_free, 1)
                for b in range(BLKS):
                    last = nc.vector.bn_stats(stats[:, b, :], y[:, b, :])
                last.then_inc(final_step, 1)

            def end_variance(g):
                dve.wait_ge(final_step, g * STEPS + 7)
                dve.sem_inc(dve_tick, 1)
                for b in range(BLKS):
                    last = nc.vector.bn_aggr(mv[:, b, :], stats[:, b, :])
                last.then_inc(final_step, 1)

            def end_eps(g):
                dve.wait_ge(final_step, g * STEPS + STEPS)
                nc.vector.tensor_scalar(rstd[:, 0:BLKS], mv[:, :, 1], EPS, None, ALU.add).then_inc(var_ready, 1)

            def end_normalize(g):
                dve.wait_ge(rstd_ready, g + 1)
                for b in range(BLKS):
                    last = nc.vector.tensor_scalar(y[:, b, :], y[:, b, :], mv[:, b, 0:1], rstd[:, b:b + 1],
                                                   ALU.subtract, ALU.mult)
                last.then_inc(y_ready, 1)

            STEPS = 8
            END = {(4, "words"): end_add_parts, (4, "end"): end_weigh,
                   (5, "compares"): end_add, (5, "words"): end_reciprocal, (5, "end"): end_divide,
                   (6, "compares"): end_residual, (6, "words"): end_moments, (6, "end"): end_variance,
                   (7, "compares"): end_eps, (7, "end"): end_normalize}

            def end_at(g, u, place):
                if g is not None and (u, place) in END:
                    END[u, place](g)

            def other_units(g, after):
                with dve.Fori(1, UNITS // BODY - 1) as i:
                    body_units(g, i, (g, i + 1))
                body_units(g, UNITS // BODY - 1, after)

            compares(0, 0, 0)
            body_units(0, 0, (0, 1))
            with dve.Fori(0, GROUPS - 1) as g:
                other_units(g, (g + 1, 0))
                body_units(g + 1, 0, (g + 1, 1), g)
            other_units(GROUPS - 1, None)
            for step in END.values():
                step(GROUPS - 1)

        @block.gpsimd
        def _(pool):
            nc.gpsimd.memset(ident[:, :], 0.0).then_inc(pool_step, 1)
            pool.wait_ge(pool_step, 1)
            nc.gpsimd.affine_select(out=ident[:, :], in_=ident[:, :], compare_op=ALU.not_equal, fill=1.0, base=0,
                                    pattern=[[-1, P]], channel_multiplier=1).then_inc(consts_ready, 1)
            nc.gpsimd.memset(halfpow[:, :], -0.5)
            nc.gpsimd.memset(hp[:, :].rearrange("p (q v) -> p q v", v=VW)[:, :, FO:VW], 1.0)
            pool.wait_ge(maxima_ready, 1)
            nc.gpsimd.partition_all_reduce(mxa[:, :], mx[:, :], P, bass.bass_isa.ReduceOp.max).then_inc(maxima_all, 1)
            pool.wait_ge(exps_scaled, 1)
            with pool.Fori(0, TILES // VT // NF) as i:
                for b in range(NF):
                    c = i * NF + b
                    pool.wait_ge(lo_ready, c + 1)
                    nc.gpsimd.tensor_tensor(
                        fval[:, b, 1, :].rearrange("p (q c) -> p q c", c=VW),
                        hp[:, bass.ds(c * FV, FV)].rearrange("p (q c) -> p q c", c=VW),
                        e2[:, bass.ds(c * VT * HEADS, VT * HEADS)].unsqueeze(2).to_broadcast([P, VT * HEADS, VW]),
                        ALU.mult).then_inc(f2_ready, 1)
            with pool.Fori(0, GROUPS) as g:
                pool.wait_ge(var_ready, g + 1)
                nc.gpsimd.tensor_tensor(rstd[:, :], rstd[:, :], halfpow[:, :], ALU.pow).then_inc(rstd_ready, 1)
                pool.wait_ge(y_ready, g + 1)
                pool.sem_inc(pool_tick, 1)
                pool.dma_start(out_t[:, bass.ds(g * BLKS, BLKS), :], y[:, :, :]).then_inc(out_stored, 16)
                pool.wait_ge(out_stored, 16 * g + 16)
                pool.sem_inc(y_free, 1)


_INS = ["x", "adj", "L0_gnn_weight", "L0_gnn_att_src", "L0_gnn_att_dst", "L0_gnn_bias"]


def kernel(**inputs):
    import numpy as np
    import concourse.bacc as bacc
    from concourse.bass_utils import run_bass_kernel_spmd

    nc = bacc.Bacc("TRN2", target_bir_lowering=False, num_devices=1)
    arrays, args = {}, []
    for name in _INS:
        a = np.ascontiguousarray(inputs[name])
        arrays[f"in_{name}"] = a
        args.append(nc.dram_tensor(f"in_{name}", a.shape, mybir.dt.from_np(a.dtype), kind="ExternalInput").ap())
    shape = arrays["in_x"].shape
    args.append(nc.dram_tensor("out", shape, mybir.dt.from_np(np.dtype("float32")), kind="ExternalOutput").ap())
    gat_residual_layernorm(nc, *args)
    r = run_bass_kernel_spmd(nc, [arrays], core_ids=[0])
    return r.results[0]["out"]
```
